# Optimizing a Trainium2 kernel written in Bass

```python
import numpy as np
import jax
import jax.numpy as jnp

def _softmax(x, axis=-1):
    return jax.nn.softmax(x, axis=axis)

def _gelu(x):
    return jax.nn.gelu(x, approximate=True)

def _silu(x):
    return jax.nn.silu(x)

def _sigmoid(x):
    return jax.nn.sigmoid(x)

def _layernorm(x, axis=-1, eps=1e-05):
    m = jnp.mean(x, axis=axis, keepdims=True)
    v = jnp.var(x, axis=axis, keepdims=True)
    return (x - m) / jnp.sqrt(v + eps)

def _scatter_add(tgt, idx, src, axis=0):
    return tgt.at[idx].add(src)

def _segment_sum(src, seg, n):
    return jax.ops.segment_sum(src, seg, n)
kernel_name = 'mk_perceiver_d1_seqx_r2_f9faf3'

def setup_inputs(seed: int=0):
    np.random.seed(seed)
    _w = jnp.asarray

    def _rec_inputs():
        import jax
        import jax.numpy as jnp
        _rk = jax.random.key(seed)
        x = 7.22e-05 + 1 * jax.random.normal(jax.random.fold_in(_rk, 1), (16, 64, 512), jnp.float32)
        _lenS = 64 - jax.random.randint(jax.random.fold_in(_rk, 7), (16,), 0, max(1, 64 // 4) + 1, jnp.int32)
        _lenS2 = 512 - jax.random.randint(jax.random.fold_in(_rk, 8), (16,), 0, max(1, 512 // 4) + 1, jnp.int32)
        _ctx_1024P = jax.random.normal(jax.random.fold_in(_rk, 11), (16, 16, 512), jnp.float32)
        _ctx_1024c = jax.random.dirichlet(jax.random.fold_in(_rk, 511), 0.3 * jnp.ones((16,), jnp.float32), (16, 512))
        _ctx_1024t = jnp.einsum('bsk,bkd->bsd', _ctx_1024c, _ctx_1024P)
        _ctx_1024t = _ctx_1024t * jax.lax.rsqrt(jnp.mean(jnp.square(_ctx_1024t)) + 1e-12) * 0.953939
        ctx_1024 = 4.13588e-05 + 0.999923 * (_ctx_1024t + 0.3 * jax.random.normal(jax.random.fold_in(_rk, 611), (16, 512, 512), jnp.float32))
        return (x, ctx_1024)
    x, ctx_1024 = _rec_inputs()

    def _L0_xattn_setup():
        import jax, jax.numpy as jnp
        import numpy as np
        N_HEAD, MODEL_DIM, KEY_DIM, VALUE_DIM = (16, 512, 64, 64)
        B, S = (4, 1024)
        EPS = 1e-05
        TEMP = float(np.sqrt(KEY_DIM))
        key = jax.random.key(seed)
        ks = jax.random.split(key, 12)
        d = {'query': jax.random.normal(ks[0], (B, S, MODEL_DIM), jnp.float32), 'key': jax.random.normal(ks[1], (B, S, MODEL_DIM), jnp.float32), 'value': jax.random.normal(ks[2], (B, S, MODEL_DIM), jnp.float32), 'Wq': jax.random.normal(ks[3], (MODEL_DIM, N_HEAD * KEY_DIM), jnp.float32) * np.sqrt(2.0 / (MODEL_DIM + KEY_DIM)), 'bq': jnp.zeros((N_HEAD * KEY_DIM,), jnp.float32), 'Wk': jax.random.normal(ks[4], (MODEL_DIM, N_HEAD * KEY_DIM), jnp.float32) * np.sqrt(2.0 / (MODEL_DIM + KEY_DIM)), 'bk': jnp.zeros((N_HEAD * KEY_DIM,), jnp.float32), 'Wv': jax.random.normal(ks[5], (MODEL_DIM, N_HEAD * VALUE_DIM), jnp.float32) * np.sqrt(2.0 / (MODEL_DIM + VALUE_DIM)), 'bv': jnp.zeros((N_HEAD * VALUE_DIM,), jnp.float32), 'Wo': jax.random.normal(ks[6], (N_HEAD * VALUE_DIM, MODEL_DIM), jnp.float32) * np.sqrt(2.0 / (N_HEAD * VALUE_DIM + MODEL_DIM)), 'bo': jnp.zeros((MODEL_DIM,), jnp.float32), 'ln_gamma': jnp.ones((MODEL_DIM,), jnp.float32), 'ln_beta': jnp.zeros((MODEL_DIM,), jnp.float32)}
        return d
    _L0_xattn_all = _L0_xattn_setup()
    _L0_xattn_in = {k: v for k, v in _L0_xattn_all.items() if k in ('Wq', 'bq', 'Wk', 'bk', 'Wv', 'bv', 'Wo', 'bo', 'ln_gamma', 'ln_beta')}
    del _L0_xattn_all

    def _L0_attn_setup():
        import jax, jax.numpy as jnp
        import numpy as np
        H = 16
        GRID = 16
        TOK_PER_FRAME = GRID * GRID

        def _rope(x, pos, dim):
            half = dim // 2
            omega = jnp.arange(half, dtype=x.dtype) / (dim / 2.0)
            inv = 1.0 / 10000.0 ** omega
            freq = pos.astype(x.dtype)[:, None] * inv
            sin = jnp.concatenate([jnp.sin(freq), jnp.sin(freq)], axis=-1)
            cos = jnp.concatenate([jnp.cos(freq), jnp.cos(freq)], axis=-1)
            y = x.reshape(*x.shape[:-1], half, 2)
            y1, y2 = (y[..., 0], y[..., 1])
            rot = jnp.stack((-y2, y1), axis=-1).reshape(x.shape)
            return x * cos + rot * sin

        def _apply_3d_rope(qk, f_ids, h_ids, w_ids, d_dim):
            s = 0
            parts = []
            for pos in (f_ids, h_ids, w_ids):
                parts.append(_rope(qk[..., s:s + d_dim], pos, d_dim))
                s += d_dim
            if s < qk.shape[-1]:
                parts.append(qk[..., s:])
            return jnp.concatenate(parts, axis=-1)
        key = jax.random.key(seed)
        ks = jax.random.split(key, 5)
        D = 512
        B, N = (4, 1024)
        sc = 0.02
        return {'hidden_states': jax.random.normal(ks[0], (B, N, D), jnp.float32), 'Wq': jax.random.normal(ks[1], (D, D), jnp.float32) * sc, 'bq': jnp.zeros((D,), jnp.float32), 'Wk': jax.random.normal(ks[2], (D, D), jnp.float32) * sc, 'bk': jnp.zeros((D,), jnp.float32), 'Wv': jax.random.normal(ks[3], (D, D), jnp.float32) * sc, 'bv': jnp.zeros((D,), jnp.float32), 'Wo': jax.random.normal(ks[4], (D, D), jnp.float32) * sc, 'bo': jnp.zeros((D,), jnp.float32)}
    _L0_attn_all = _L0_attn_setup()
    _L0_attn_in = {k: v for k, v in _L0_attn_all.items() if k in ('Wq', 'bq', 'Wk', 'bk', 'Wv', 'bv', 'Wo', 'bo')}
    del _L0_attn_all

    def _L0_ffn_setup():
        import jax, jax.numpy as jnp
        import numpy as np
        from jax import lax
        D = 512
        H = 2048
        E = 8
        TOPK = 2
        key = jax.random.key(seed)
        ks = jax.random.split(key, 7)
        s = 0.02
        return {'x': jax.random.normal(ks[0], (2, 1024, D), dtype=jnp.float32), 'W1': jax.random.normal(ks[1], (E, D, H), dtype=jnp.float32) * s, 'b1': jnp.zeros((E, H), dtype=jnp.float32), 'W2': jax.random.normal(ks[2], (E, H, D), dtype=jnp.float32) * s, 'b2': jnp.zeros((E, D), dtype=jnp.float32), 'Wr': jax.random.normal(ks[3], (D, E), dtype=jnp.float32) * s, 'br': jnp.zeros((E,), dtype=jnp.float32)}
    _L0_ffn_all = _L0_ffn_setup()
    _L0_ffn_in = {k: v for k, v in _L0_ffn_all.items() if k in ('W1', 'b1', 'W2', 'b2', 'Wr', 'br')}
    del _L0_ffn_all
    return {'x': x, 'ctx_1024': ctx_1024, 'L0_xattn_Wq': _L0_xattn_in['Wq'], 'L0_xattn_bq': _L0_xattn_in['bq'], 'L0_xattn_Wk': _L0_xattn_in['Wk'], 'L0_xattn_bk': _L0_xattn_in['bk'], 'L0_xattn_Wv': _L0_xattn_in['Wv'], 'L0_xattn_bv': _L0_xattn_in['bv'], 'L0_xattn_Wo': _L0_xattn_in['Wo'], 'L0_xattn_bo': _L0_xattn_in['bo'], 'L0_xattn_ln_gamma': _L0_xattn_in['ln_gamma'], 'L0_xattn_ln_beta': _L0_xattn_in['ln_beta'], 'L0_attn_Wq': _L0_attn_in['Wq'], 'L0_attn_bq': _L0_attn_in['bq'], 'L0_attn_Wk': _L0_attn_in['Wk'], 'L0_attn_bk': _L0_attn_in['bk'], 'L0_attn_Wv': _L0_attn_in['Wv'], 'L0_attn_bv': _L0_attn_in['bv'], 'L0_attn_Wo': _L0_attn_in['Wo'], 'L0_attn_bo': _L0_attn_in['bo'], 'L0_ffn_W1': _L0_ffn_in['W1'], 'L0_ffn_b1': _L0_ffn_in['b1'], 'L0_ffn_W2': _L0_ffn_in['W2'], 'L0_ffn_b2': _L0_ffn_in['b2'], 'L0_ffn_Wr': _L0_ffn_in['Wr'], 'L0_ffn_br': _L0_ffn_in['br']}

def reference(x, ctx_1024, L0_xattn_Wq, L0_xattn_bq, L0_xattn_Wk, L0_xattn_bk, L0_xattn_Wv, L0_xattn_bv, L0_xattn_Wo, L0_xattn_bo, L0_xattn_ln_gamma, L0_xattn_ln_beta, L0_attn_Wq, L0_attn_bq, L0_attn_Wk, L0_attn_bk, L0_attn_Wv, L0_attn_bv, L0_attn_Wo, L0_attn_bo, L0_ffn_W1, L0_ffn_b1, L0_ffn_W2, L0_ffn_b2, L0_ffn_Wr, L0_ffn_br):
    import jax
    import jax.numpy as jnp

    def _L0_xattn_ref(query, key, value, Wq, bq, Wk, bk, Wv, bv, Wo, bo, ln_gamma, ln_beta):
        import jax, jax.numpy as jnp
        import numpy as np
        N_HEAD, MODEL_DIM, KEY_DIM, VALUE_DIM = (16, 512, 64, 64)
        B, S = (4, 1024)
        EPS = 1e-05
        TEMP = float(np.sqrt(KEY_DIM))
        b, sq, _ = query.shape
        residual = query
        q = (query @ Wq + bq).reshape(b, sq, N_HEAD, KEY_DIM)
        k = (key @ Wk + bk).reshape(b, key.shape[1], N_HEAD, KEY_DIM)
        v = (value @ Wv + bv).reshape(b, value.shape[1], N_HEAD, VALUE_DIM)
        scores = jnp.einsum('bqhd,bkhd->bhqk', q, k) / TEMP
        attn = jax.nn.softmax(scores, axis=-1)
        out = jnp.einsum('bhqk,bkhd->bqhd', attn, v).reshape(b, sq, N_HEAD * VALUE_DIM)
        out = out @ Wo + bo + residual
        mu = jnp.mean(out, axis=-1, keepdims=True)
        var = jnp.var(out, axis=-1, keepdims=True)
        return (out - mu) * jax.lax.rsqrt(var + EPS) * ln_gamma + ln_beta

    def _L0_attn_ref(hidden_states, Wq, bq, Wk, bk, Wv, bv, Wo, bo):
        import jax, jax.numpy as jnp
        import numpy as np
        H = 16
        GRID = 16
        TOK_PER_FRAME = GRID * GRID

        def _rope(x, pos, dim):
            half = dim // 2
            omega = jnp.arange(half, dtype=x.dtype) / (dim / 2.0)
            inv = 1.0 / 10000.0 ** omega
            freq = pos.astype(x.dtype)[:, None] * inv
            sin = jnp.concatenate([jnp.sin(freq), jnp.sin(freq)], axis=-1)
            cos = jnp.concatenate([jnp.cos(freq), jnp.cos(freq)], axis=-1)
            y = x.reshape(*x.shape[:-1], half, 2)
            y1, y2 = (y[..., 0], y[..., 1])
            rot = jnp.stack((-y2, y1), axis=-1).reshape(x.shape)
            return x * cos + rot * sin

        def _apply_3d_rope(qk, f_ids, h_ids, w_ids, d_dim):
            s = 0
            parts = []
            for pos in (f_ids, h_ids, w_ids):
                parts.append(_rope(qk[..., s:s + d_dim], pos, d_dim))
                s += d_dim
            if s < qk.shape[-1]:
                parts.append(qk[..., s:])
            return jnp.concatenate(parts, axis=-1)
        B, N, D = hidden_states.shape
        hd = D // H
        d_dim = 2 * (hd // 3 // 2)

        def heads(x):
            return x.reshape(B, N, H, hd).transpose(0, 2, 1, 3)
        q = heads(hidden_states @ Wq + bq)
        k = heads(hidden_states @ Wk + bk)
        v = heads(hidden_states @ Wv + bv)
        ids = jnp.arange(N)
        f_ids = ids // TOK_PER_FRAME
        rem = ids - TOK_PER_FRAME * f_ids
        h_ids = rem // GRID
        w_ids = rem - GRID * h_ids
        q = _apply_3d_rope(q, f_ids, h_ids, w_ids, d_dim)
        k = _apply_3d_rope(k, f_ids, h_ids, w_ids, d_dim)
        scale = hd ** (-0.5)
        attn = jnp.einsum('bhqd,bhkd->bhqk', q, k) * scale
        attn = jax.nn.softmax(attn.astype(jnp.float32), axis=-1).astype(q.dtype)
        ctx = jnp.einsum('bhqk,bhkd->bhqd', attn, v)
        ctx = ctx.transpose(0, 2, 1, 3).reshape(B, N, D)
        return ctx @ Wo + bo

    def _L0_ffn_ref(x, W1, b1, W2, b2, Wr, br):
        import jax, jax.numpy as jnp
        import numpy as np
        from jax import lax
        D = 512
        H = 2048
        E = 8
        TOPK = 2
        B, S, _ = x.shape
        xf = x.reshape(-1, D)
        logits = xf @ Wr + br
        topv, _ = lax.top_k(logits, TOPK)
        thresh = topv[:, TOPK - 1:TOPK]
        masked = jnp.where(logits >= thresh, logits, -jnp.inf)
        weights = jax.nn.softmax(masked, axis=-1)
        h = jax.nn.gelu(jnp.einsum('td,edh->eth', xf, W1) + b1[:, None, :], approximate=False)
        expert_out = jnp.einsum('eth,ehd->etd', h, W2) + b2[:, None, :]
        out = jnp.einsum('etd,te->td', expert_out, weights)
        return out.reshape(B, S, D)
    x = x + _L0_xattn_ref(_layernorm(x, axis=-1), ctx_1024, ctx_1024, L0_xattn_Wq, L0_xattn_bq, L0_xattn_Wk, L0_xattn_bk, L0_xattn_Wv, L0_xattn_bv, L0_xattn_Wo, L0_xattn_bo, L0_xattn_ln_gamma, L0_xattn_ln_beta)
    x = x + _L0_attn_ref(_layernorm(x, axis=-1), L0_attn_Wq, L0_attn_bq, L0_attn_Wk, L0_attn_bk, L0_attn_Wv, L0_attn_bv, L0_attn_Wo, L0_attn_bo)
    x = x + _L0_ffn_ref(_layernorm(x, axis=-1), L0_ffn_W1, L0_ffn_b1, L0_ffn_W2, L0_ffn_b2, L0_ffn_Wr, L0_ffn_br)
    return x

_drawn_inputs = setup_inputs


def setup_inputs(seed=0):
    import zlib

    import numpy as np

    out = dict(_drawn_inputs(seed))
    spreads = {'L0_xattn_bq': (0.0, 0.286),
     'L0_xattn_bk': (0.0, 2.0),
     'L0_xattn_bv': (0.0, 0.1),
     'L0_xattn_bo': (0.0, 0.1),
     'L0_xattn_ln_gamma': (1.0, 0.2),
     'L0_xattn_ln_beta': (0.0, 0.1),
     'L0_attn_bq': (0.0, 0.8),
     'L0_attn_bk': (0.0, 2.0),
     'L0_attn_bv': (0.0, 0.302),
     'L0_attn_bo': (0.0, 0.1),
     'L0_ffn_b1': (0.0, 0.397),
     'L0_ffn_b2': (0.0, 0.1),
     'L0_ffn_br': (0.0, 0.1)}
    factors = {'L0_attn_Wq': 8.0, 'L0_attn_Wk': 8.0}
    for name, (base, spread) in spreads.items():
        noise = np.random.default_rng([zlib.crc32(name.encode()), seed]).standard_normal(out[name].shape)
        drawn = base * np.exp(spread * noise) if base else spread * noise
        out[name] = jnp.asarray(drawn.astype(out[name].dtype))
    for name, factor in factors.items():
        out[name] = (out[name] * factor).astype(out[name].dtype)
    return out
```

```python
from contextlib import ExitStack

import numpy as np

import concourse.bass as bass
from concourse import mybir

F32 = mybir.dt.float32
F32R = mybir.dt.float32r
ALU = mybir.AluOpType
ACT = mybir.ActivationFunctionType
AX = mybir.AxisListType.X
KB = 1024
P = 128


class Stage:

    def __init__(self, sem, step):
        self.sem, self.step, self.count = sem, step, 0

    def ticket(self):
        self.count += self.step
        return (self, self.count)


class Program:

    def __init__(self, nc, stack):
        self.nc, self.stack = nc, stack
        self.lists = {e: [] for e in ("sync", "tensor", "vector", "scalar", "gpsimd")}
        self.stages = {}

    def stage(self, name, step):
        if name not in self.stages:
            self.stages[name] = Stage(self.stack.enter_context(self.nc.semaphore(name)), step)
        return self.stages[name]

    def run(self, engine, stage, waits, emit):
        s = self.stage(stage, 16 if engine == "sync" else 1)
        t = s.ticket()
        self.lists[engine].append((tuple(w for w in waits if w), emit, s))
        return t

    def close(self, engine, waits):
        self.lists[engine].append((tuple(waits), None, None))

    def emit_all(self, block):
        def body(name):
            def emit(eng):
                reached = {}
                for waits, fn, stage in self.lists[name]:
                    for s, v in waits:
                        if reached.get(id(s), 0) < v:
                            eng.wait_ge(s.sem, v)
                            reached[id(s)] = v
                    if fn is not None:
                        fn(eng).then_inc(stage.sem, stage.step)
            return emit

        for name in self.lists:
            if self.lists[name]:
                body_fn = body(name)
                {"sync": block.sync, "tensor": block.tensor, "vector": block.vector,
                 "scalar": block.scalar, "gpsimd": block.gpsimd}[name](body_fn)


def perceiver_block(nc, a, out):
    B, TB, D = 16, 64, 512
    T = B * TB
    NT = T // P
    KD = D // P
    NKEY = 512
    H1, HD1 = 16, 64
    HV = H1 * HD1
    NJ = HV // P
    NKT = NKEY // P
    H2, HD2 = 16, 32
    E, HID = 8, 2048
    NI = HID // P
    EPS = 1e-5
    SCALE1 = HD1 ** -0.5
    SCALE2 = HD2 ** -0.5

    with ExitStack() as stack:
        pg = Program(nc, stack)
        run = pg.run
        base = -(-nc.sbuf_base // 64) * 64

        def place(name, kb, shape, dt=F32):
            return nc.alloc_sbuf_tensor_at(name, shape, dt, offset=base + int(kb * KB))

        bank = [stack.enter_context(nc.psum_tensor(f"bank{i}", [P, 512], F32)) for i in range(8)]

        ident = place("ident", 0, [P, P])
        b1c = place("b1c", 0.5, [P, E * NI])
        bqc = place("bqc", 1, [P, NJ])
        bqs = place("bqs", 1 + 1 / 32, [P, NJ])
        bkc = place("bkc", 1 + 2 / 32, [P, NJ])
        mv = place("mv", 1 + 3 / 32, [P, NT, 2])
        rstd = place("rstd", 1 + 5 / 32, [P, NT])
        nmr = place("nmr", 1 + 6 / 32, [P, NT])
        bst = place("bst", 1 + 7 / 32, [P, 2, 6])
        mv2 = place("mv2", 1 + 9 / 32, [P, 2, 2])
        rstd2 = place("rstd2", 1 + 10 / 32, [P, 2, 2])
        smn = place("smn", 1 + 11 / 32, [P, 3])
        ssum = place("ssum", 1 + 12 / 32, [P, 3])
        srec = place("srec", 1 + 13 / 32, [P, 3])
        mx2 = place("mx2", 1 + 14 / 32, [P, 2, 8])
        sm2 = place("sm2", 1 + 16 / 32, [P, 2, 8])
        rc2 = place("rc2", 1 + 18 / 32, [P, 2, 8])
        wgt = place("wgt", 1 + 20 / 32, [P, NT, E])
        mhalf = place("mhalf", 1 + 29 / 32, [P, 2])
        brb = place("brb", 1 + 28 / 32, [P, E])
        rt = place("rt", 2, [P, 6, E])
        wr = place("wr", 2.25, [P, KD, E])
        wT = place("wT", 2.5, [E, P])
        c0 = 3
        QO = place("QO", c0, [P, NJ, T])
        raw = [place(f"raw{i}", c0 + 96 + 4 * i, [P, 1024]) for i in range(3)]
        Wk = [place(f"Wk{i}", c0 + 32 + 16 * i, [P, KD, HV], F32R) for i in range(2)]
        Wv = [place(f"Wv{i}", c0 + 64 + 16 * i, [P, KD, HV], F32R) for i in range(2)]
        o = c0 + 108
        ctx = [[place(f"ctx{r}{i}", o + 16 * r + 8 * i, [P, KD, NKEY], F32R) for i in range(2)] for r in range(2)]
        xs = place("xs", o + 16, [P, NT, D])
        xnT = [place(f"xnT{i}", o + 32 + 16 * i, [P, KD, T], F32R) for i in range(2)]
        Wq = [place(f"Wq{i}", o + 64 + 16 * i, [P, KD, HV], F32R) for i in range(2)]
        qbd = [[place(f"qbd{r}{i}", o + 32 + 8 * r + 4 * i, [P, NJ, P], F32R) for i in range(2)] for r in range(2)]
        kT = [[place(f"kT{r}{i}", o + 48 + 4 * r + 2 * i, [P, NKEY], F32R) for i in range(2)] for r in range(2)]
        V = [place(f"V{r}", o + 56 + 8 * r, [P, NKT, 512]) for r in range(3)]
        Pr = [place(f"Pr{r}", o + 80 + 2 * r, [P, NKEY]) for r in range(2)]
        PT = [place(f"PT{r}", o + 84 + 2 * r, [P, NKEY]) for r in range(2)]
        bvb = place("bvb", o + 88, [P, HV])
        Wo = [place(f"Wo{i}", c0 + 64 + 16 * i, [P, NJ, D], F32R) for i in range(2)]
        oT = [[place(f"oT{r}{i}", o + 8 * r + 4 * i, [P, NJ, P], F32R) for i in range(2)] for r in range(2)]
        x1 = place("x1", c0 + 32, [P, NT, D])
        bob = place("bob", c0 + 48, [P, D])
        gab = place("gab", c0 + 50, [P, D])
        beb = place("beb", c0 + 52, [P, D])
        xr = [place(f"xr{r}", c0 + 54 + 2 * r, [P, D]) for r in range(2)]
        ya = [place(f"ya{r}", c0 + 58 + 2 * r, [P, D]) for r in range(2)]
        Wa = [[place(f"Wa{w}{i}", o + 16 + 16 * w + 8 * i, [P, KD, D], F32R) for i in range(2)] for w in range(4)]
        s0 = c0 + 48
        absb = [place(f"absb{w}", s0 + 2 * w, [P, D]) for w in range(4)]
        cosb = place("cosb", s0 + 8, [P, D])
        sinb = place("sinb", s0 + 10, [P, D])
        nx = [place(f"nx{r}", s0 + 12 + 2 * r, [P, D]) for r in range(2)]
        nxT = [[place(f"nxT{r}{i}", s0 + 16 + 4 * r + 2 * i, [P, KD, P], F32R) for i in range(2)] for r in range(2)]
        qk = [place(f"qk{w}", s0 + 24 + 2 * w, [P, D]) for w in range(2)]
        rtmp = [place(f"rtmp{w}", s0 + 28 + 2 * w, [P, D]) for w in range(2)]
        vn = [place(f"vn{r}", s0 + 32 + 2 * r, [P, D]) for r in range(2)]
        kT2 = [place(f"kT2{r}", s0 + 36 + 2 * r, [P, KD, P]) for r in range(2)]
        P2 = [place(f"P2{r}", s0 + 40 + 2 * r, [P, 8, TB]) for r in range(2)]
        PT2 = [place(f"PT2{r}", s0 + 44 + 2 * r, [P, D]) for r in range(2)]
        s1 = o
        qbd2 = [place(f"qbd2{r}", s1 + 8 * r, [P, 2, 8, P]) for r in range(2)]
        s2 = o + 80
        Vbd = [place(f"Vbd{r}", s2 + 4 * r, [P, 2, 4, P]) for r in range(2)]
        o2f = place("o2f", s2 + 8, [P, 4, P])
        o2 = [place(f"o2{i}", s2 + 10 + 2 * i, [P, 4, P], F32R) for i in range(2)]
        x2T = [place(f"x2T{i}", c0 + 16 * i, [P, KD, T], F32R) for i in range(2)]
        b2s = place("b2s", s2 + 14, [E, D])
        slots = [c0 + 48 + 8 * i for i in range(6)] + [o + 8 * i for i in range(10)]
        Wh = [[place(f"Wh{s}{i}", kb + 4 * i, [P, 1024], F32R) for i in range(2)] for s, kb in enumerate(slots)]
        e0 = o + 80
        gl = [place(f"gl{r}", e0 + 2 * r, [P, 512]) for r in range(2)]
        hs = [[place(f"hs{r}{i}", e0 + 4 + 4 * r + 2 * i, [P, 512], F32R) for i in range(2)] for r in range(2)]

        def dma(stage, dst, src, *waits):
            return run("sync", stage, waits, lambda e: e.dma_start(dst, src))

        def copy_act(stage, dst, src, *waits, **kw):
            return run("scalar", stage, waits, lambda e: e.activation(dst, src, ACT.Copy, **kw))

        def tt(engine, stage, dst, x, y, op, *waits):
            return run(engine, stage, waits, lambda e: e.tensor_tensor(dst, x, y, op))

        def products(stage, dst, pairs, *waits):
            def emit(e):
                for n, (l, r) in enumerate(pairs):
                    mm = e.matmul(dst, l, r, start=n == 0, stop=n == len(pairs) - 1)
                return mm
            return run("tensor", stage, waits, emit)

        def split_pairs(lhs, rhs):
            return [p for (lh, ll), (rh, rl) in zip(lhs, rhs) for p in ((lh, rh), (lh, rl), (ll, rh))]

        def transposes(stage, dst, srcs, *waits):
            def emit(e):
                for n, s in enumerate(srcs):
                    mm = e.transpose(dst[:, n * P:(n + 1) * P], s, ident[:])
                return mm
            return run("tensor", stage, waits, emit)

        raw_used = [None] * 3
        raw_n = [0]

        def load_split(src, hi, lo, lo_engine, *waits):
            n = raw_n[0]
            raw_n[0] += 1
            r = raw[n % 3]
            shaped = r[:] if len(src.shape) == 2 else r[:].rearrange("p (a b) -> p a b", a=src.shape[1])
            got = dma(f"raw_loaded{n % 3}", shaped, src, raw_used[n % 3])
            h = copy_act("split_hi", hi, shaped, got, *waits)
            t = tt(lo_engine, f"split_lo_{lo_engine}", lo, shaped, hi, ALU.subtract, h)
            raw_used[n % 3] = t
            return t

        def layernorm(stage, src, dst, ring, *waits):
            st, m, r = bst[:, ring, :], mv2[:, ring, :], rstd2[:, ring, :]
            t = run("vector", "ln_small", waits, lambda e: e.bn_stats(st, src))
            t = run("vector", "ln_small", [t], lambda e: e.bn_aggr(m, st))
            t = run("vector", "ln_small", [t], lambda e: e.tensor_scalar(r[:, 0:1], m[:, 1:2], EPS, None, ALU.add))
            t = tt("gpsimd", "ln_pow", r[:, 0:1], r[:, 0:1], mhalf[:, 0:1], ALU.pow, t, t_mhalf)
            t = run("vector", "ln_small", [t], lambda e: e.scalar_tensor_tensor(r[:, 1:2], m[:, 0:1], -1.0, r[:, 0:1], ALU.mult, ALU.mult))
            return run("vector", stage, [t], lambda e: e.tensor_scalar(dst, src, r[:, 0:1], r[:, 1:2], ALU.mult, ALU.add))

        x_in = a["x"].rearrange("(t p) d -> p t d", p=P)
        t_mhalf = run("gpsimd", "mhalf", [], lambda e: e.memset(mhalf[:], -0.5))
        t_ident = dma("const_ident", ident[:], a["ident"])
        x_got = [dma(f"x_loaded{h}", xs[:, 2 * h:2 * h + 2, :], x_in[:, 2 * h:2 * h + 2, :]) for h in range(4)]
        for dst, name in ((bqc, "bq"), (bkc, "bk"), (b1c, "b1")):
            t_cols = dma("const_columns", dst[:], a[name])
        t_bqs = run("vector", "bq_scaled", [t_cols], lambda e: e.tensor_scalar(bqs[:], bqc[:], SCALE1, None, ALU.mult))

        t_wq = [load_split(a["Wq"][k * P:(k + 1) * P, :], Wq[0][:, k, :], Wq[1][:, k, :], "vector" if k % 2 else "gpsimd") for k in range(KD)]

        def load_ctx(b, *waits):
            for c in range(2):
                t = load_split(a["ctxT"][b, :, 2 * c:2 * c + 2, :], ctx[b % 2][0][:, 2 * c:2 * c + 2, :],
                               ctx[b % 2][1][:, 2 * c:2 * c + 2, :], "gpsimd", *waits)
            return t

        xnT_done = []
        lo_prev = [None, None]
        for h in range(4):
            for t in (2 * h, 2 * h + 1):
                st = run("vector", "x_stats", [x_got[h], pg_last if t else None],
                         lambda e, t=t: e.bn_stats(bst[:, t % 2, :], xs[:, t, :]))
                pg_last = run("vector", "x_stats", [st], lambda e, t=t: e.bn_aggr(mv[:, t, :], bst[:, t % 2, :]))
            s = slice(2 * h, 2 * h + 2)
            r = run("vector", "x_stats", [pg_last], lambda e, s=s: e.tensor_scalar(rstd[:, s], mv[:, s, 1], EPS, None, ALU.add))
            r = tt("gpsimd", "x_pow", rstd[:, s], rstd[:, s], mhalf[:], ALU.pow, r, t_mhalf)
            r = run("vector", "x_stats", [r], lambda e, s=s: e.scalar_tensor_tensor(nmr[:, s], mv[:, s, 0], -1.0, rstd[:, s], ALU.mult, ALU.mult))
            for t in (2 * h, 2 * h + 1):
                xn = run("vector", "x_normal", [r], lambda e, t=t: e.tensor_scalar(
                    xs[:, t, :], xs[:, t, :], rstd[:, t:t + 1], nmr[:, t:t + 1], ALU.mult, ALU.add))
                tr = transposes("xnT_psum", bank[t % 2], [xs[:, t, k * P:(k + 1) * P] for k in range(KD)],
                                xn, t_ident, lo_prev[t % 2])
                src = bank[t % 2][:].rearrange("p (k q) -> p k q", k=KD)
                dst = [x[:, :, t * P:(t + 1) * P] for x in xnT]
                hi = copy_act("xnT_hi", dst[0], src, tr)
                lo_prev[t % 2] = tt("vector", "xnT_lo", dst[1], src, dst[0], ALU.subtract, hi)
                xnT_done.append(lo_prev[t % 2])
        q_evac = [None, None]
        for half in range(2):
            c = slice(half * 512, half * 512 + 512)
            for j in range(NJ):
                n = half * NJ + j
                js = slice(j * P, (j + 1) * P)
                q_psum = products("q_psum", bank[2 + n % 2][:],
                                  split_pairs([(Wq[0][:, k, js], Wq[1][:, k, js]) for k in range(KD)],
                                              [(xnT[0][:, k, c], xnT[1][:, k, c]) for k in range(KD)]),
                                  *t_wq[2:], xnT_done[4 * half + 3], q_evac[n % 2])
                q_evac[n % 2] = run("scalar", "q_done", [q_psum, t_bqs], lambda e, n=n, j=j, c=c: e.activation(
                    QO[:, j, c], bank[2 + n % 2][:], ACT.Identity, bias=bqs[:, j:j + 1], scale=SCALE1))
        q_all = q_evac[1]
        a_done = q_psum

        t_ctx = {0: load_ctx(0)}
        for k in range(KD):
            t_wv = load_split(a["Wv"][k * P:(k + 1) * P, :], Wv[0][:, k, :], Wv[1][:, k, :], "gpsimd" if k % 2 else "vector")
            t_wv2 = t_wv if k == KD - 2 else (t_wv2 if k == KD - 1 else None)
        for k in range(KD):
            t_wk = load_split(a["Wk"][k * P:(k + 1) * P, :], Wk[0][:, k, :], Wk[1][:, k, :], "gpsimd" if k % 2 else "vector")
            t_wk2 = t_wk if k == KD - 2 else (t_wk2 if k == KD - 1 else None)
        w_ready = {"v": (t_wv, t_wv2), "k": (t_wk, t_wk2)}
        t_bvb = dma("const_bv", bvb[:], a["bv"].partition_broadcast(P), a_done)
        for r in range(2):
            for i in range(2):
                t_zero = run("gpsimd", "qbd_zero", [a_done], lambda e, r=r, i=i: e.memset(qbd[r][i][:].bitcast(F32), 0.0))

        NS = B * NJ
        HALF = NJ // 2
        k_free = [None, None]
        v_free = [None, None]
        s_free = [None, None]
        t_free = o_free = None
        k_ready, v_ready, p_ready, pt_ready, qbd_ready = {}, {}, {}, {}, {}
        s_done, pt_read, pv_done, tr_done, kp_done, vp_done = {}, {}, {}, {}, {}, {}
        ov = [None]

        def pair(x, *idx):
            return (x[0][idx], x[1][idx])

        def build_qbd(b):
            r = b % 2
            before = s_done.get((b - 2) * NJ + NJ - 1)
            for h in range(2):
                rows, cols = slice(64 * h, 64 * h + 64), slice(64 * h, 64 * h + 64)
                src = QO[rows, :, b * TB:(b + 1) * TB]
                hi = copy_act("qbd_hi", qbd[r][0][rows, :, cols], src, q_all, t_zero, before)
                t = tt("vector", "qbd_lo", qbd[r][1][rows, :, cols], src, qbd[r][0][rows, :, cols], ALU.subtract, hi, t_zero, before)
            qbd_ready[b] = t

        def project_v(n):
            u, kt = divmod(n, HALF)
            b, g = divmod(u, 2)
            cs = slice(g * 512, g * 512 + 512)
            ks = slice(kt * P, (kt + 1) * P)
            bk = bank[2 + n % 2]
            ps = products("v_psum", bk[:], split_pairs([pair(ctx[b % 2], slice(None), k, ks) for k in range(KD)],
                                                      [pair(Wv, slice(None), k, cs) for k in range(KD)]),
                          t_ctx[b], *w_ready["v"], v_free[n % 2])
            v_free[n % 2] = v_ready[n] = tt("vector", "v_done", V[u % 3][:, kt, :], bk[:], bvb[:, cs], ALU.add,
                                            ps, t_bvb, pv_done.get(HALF * (u - 3) + HALF - 1))
            vp_done[n] = ps

        def project_k(n):
            b, j = divmod(n, NJ)
            js = slice(j * P, (j + 1) * P)
            bk = bank[n % 2]
            ps = products("k_psum", bk[:], split_pairs([pair(Wk, slice(None), k, js) for k in range(KD)],
                                                      [pair(ctx[b % 2], slice(None), k) for k in range(KD)]),
                          t_ctx[b], *w_ready["k"], k_free[n % 2])
            dst = kT[n % 2]
            hi = run("scalar", "k_hi", [ps, t_cols, s_done.get(n - 2), a_done], lambda e: e.activation(
                dst[0][:], bk[:], ACT.Identity, bias=bkc[:, j:j + 1]))
            k_free[n % 2] = k_ready[n] = run("vector", "k_lo", [hi], lambda e: e.scalar_tensor_tensor(
                dst[1][:], bk[:], bkc[:, j:j + 1], dst[0][:], ALU.add, ALU.subtract))
            kp_done[n] = ps

        def scores(n):
            b, j = divmod(n, NJ)
            bk = bank[4 + n % 2]
            s_done[n] = products("s_psum", bk[:], split_pairs([pair(qbd[b % 2], slice(None), j)], [(kT[n % 2][0][:], kT[n % 2][1][:])]),
                                 qbd_ready[b], k_ready[n], s_free[n % 2])
            r = n % 3
            mx = run("vector", "s_max", [s_done[n], tr_done.get(n - 3)], lambda e: e.tensor_reduce(smn[:, r:r + 1], bk[:], AX, ALU.max, negate=True))
            ex = run("scalar", "s_exp", [mx, tr_done.get(n - 2), a_done], lambda e: e.activation(
                Pr[n % 2][:], bk[:], ACT.Exp, bias=smn[:, r:r + 1], accum_out=ssum[:, r:r + 1]))
            s_free[n % 2] = ex
            rc = run("vector", "s_recip", [ex], lambda e: e.reciprocal(srec[:, r:r + 1], ssum[:, r:r + 1]))
            p_ready[n] = run("vector", "p_done", [rc], lambda e: e.tensor_scalar(Pr[n % 2][:], Pr[n % 2][:], srec[:, r:r + 1], None, ALU.mult))

        def turn(n):
            nonlocal t_free
            tr_done[n] = transposes("pT_psum", bank[6], [Pr[n % 2][:, k * P:(k + 1) * P] for k in range(NKT)], p_ready[n], t_free)
            t_free = pt_ready[n] = copy_act("pT_done", PT[n % 2][:], bank[6][:], tr_done[n], pv_done.get(n - 2))

        def weigh(n):
            nonlocal o_free
            b, j = divmod(n, NJ)
            u, s = divmod(n, HALF)
            pv_done[n] = products("o_psum", bank[7][:, 0:P],
                                  [(V[u % 3][:, kt, s * P:(s + 1) * P], PT[n % 2][:, kt * P:(kt + 1) * P]) for kt in range(NKT)],
                                  pt_ready[n], v_ready[HALF * u + HALF - 1], o_free)
            for h in range(2):
                rs = slice(64 * h, 64 * h + 64)
                o_free = copy_act("o_done", QO[rs, j, b * TB:(b + 1) * TB], bank[7][rs, rs], pv_done[n], qbd_ready[b])

        build_qbd(0)
        for n in range(HALF):
            project_v(n)
        for n in range(NS + 3):
            b, j = divmod(n, NJ)
            if n < NS:
                if j == 0 and b + 1 < B:
                    t_ctx[b + 1] = load_ctx(b + 1, kp_done.get(n - 1), vp_done.get(n - 1 - HALF + HALF), a_done)
                project_k(n)
            if 0 <= n - 1 < NS:
                scores(n - 1)
            if n + HALF < NS:
                project_v(n + HALF)
            if n < NS and j == 2 and b + 1 < B:
                build_qbd(b + 1)
            if 0 <= n - 2 < NS:
                turn(n - 2)
            if 0 <= n - 3 < NS:
                weigh(n - 3)
        o_all = o_free
        k_last, v_last = kp_done[NS - 1], vp_done[NS - 1]
        b_done = pv_done[NS - 1]

        wo_in = a["Wo"].rearrange("(j p) n -> p j n", p=P)
        for c in range(4):
            t = load_split(wo_in[:, 2 * c:2 * c + 2, :], Wo[0][:, 2 * c:2 * c + 2, :], Wo[1][:, 2 * c:2 * c + 2, :],
                           "gpsimd" if c % 2 else "vector", v_last)
            t_wo2, t_wo = (t_wo, t) if c else (None, t)
        for dst, name in ((bob, "bo"), (gab, "gamma"), (beb, "beta")):
            t_cvec = dma("const_c", dst[:], a[name].partition_broadcast(P), k_last)
        t_wa = []

        def load_wa(w):
            src = a[("aWq", "aWk", "aWv", "aWo")[w]].rearrange("(k p) n -> p k n", p=P)
            for c in range(2):
                cs = slice(2 * c, 2 * c + 2)
                t_wa.append(load_split(src[:, cs, :], Wa[w][0][:, cs, :], Wa[w][1][:, cs, :], "gpsimd", b_done, k_last))

        oT_free = [None, None]
        c_free = [None, None]
        ya_free = [None, None]
        x1_done = []
        for t in range(NT):
            ts = slice(t * P, (t + 1) * P)
            r = t % 2
            got = dma(f"xr_loaded{r}", xr[r][:], x_in[:, t, :], k_last, x1_done[t - 2] if t > 1 else None)
            hi = copy_act("oT_hi", oT[r][0][:], QO[:, :, ts], o_all, oT_free[r], k_last)
            lo = tt("vector", "oT_lo", oT[r][1][:], QO[:, :, ts], oT[r][0][:], ALU.subtract, hi)
            ps = products("c_psum", bank[r][:], split_pairs([pair(oT[r], slice(None), j) for j in range(NJ)],
                                                           [pair(Wo, slice(None), j) for j in range(NJ)]),
                          lo, t_wo, t_wo2, c_free[r], k_free[r])
            oT_free[r] = ps
            y = ya[r]
            res = run("vector", "c_res", [got, ya_free[r], k_last], lambda e, t=t, r=r, y=y: e.tensor_scalar(
                y[:], xr[r][:], rstd[:, t:t + 1], nmr[:, t:t + 1], ALU.mult, ALU.add))
            res = tt("gpsimd", "c_bias", y[:], y[:], bob[:], ALU.add, res, t_cvec)
            s = tt("vector", "c_sum", y[:], bank[r][:], y[:], ALU.add, res, ps)
            c_free[r] = s
            s = layernorm("c_norm", y[:], y[:], r, s)
            s = tt("gpsimd", "c_gamma", y[:], y[:], gab[:], ALU.mult, s)
            s = tt("gpsimd", "c_beta", y[:], y[:], beb[:], ALU.add, s)
            s = tt("vector", "x1_done", x1[:, t, :], y[:], xr[r][:], ALU.add, s, k_last)
            ya_free[r] = s
            x1_done.append(s)
            if t % 2 == 0:
                load_wa(t // 2)
        c_done = [x1_done[-1], ps]

        for w in range(4):
            t_d = dma("const_d", absb[w][:], a[("abq", "abk", "abv", "abo")[w]].partition_broadcast(P), *c_done)
        t_d = dma("const_d", cosb[:], a["cos"], *c_done)
        t_d = dma("const_d", sinb[:], a["sin"], *c_done)
        t_d = dma("const_d", brb[:], a["br"].partition_broadcast(P))
        t_d = dma("const_d", wr[:], a["Wr"].rearrange("(k p) e -> p k e", p=P))
        t_d = dma("const_d", b2s[:], a["b2"], b_done)
        for r in range(2):
            t_z2 = run("gpsimd", "d_zero", c_done, lambda e, r=r: e.memset(qbd2[r][:], 0.0))
            t_z2 = run("gpsimd", "d_zero", c_done + [b_done], lambda e, r=r: e.memset(Vbd[r][:], 0.0))

        nxT_ready, qkv, rope_done, qb_ready, kt2_ready, vbd_ready = {}, {}, {}, {}, {}, {}
        s2_done, p2_ready, pt2_done, o2_ready, x2_done, nxT_read, q3_done = {}, {}, {}, {}, {}, {}, {}
        bank0 = list(c_done)
        free = {i: list(c_done) for i in range(8)}
        tr2_done, pv2_done, out_done, lg_done, qk_read, qkT_done = {}, {}, {}, {}, {}, {}
        pt2_ready, x2T_ready, v2_ready = {}, {}, {}
        acc = x1

        def d_norm(t):
            r = t % 2
            n = layernorm("d_norm", x1[:, t, :], nx[0][:], 0, x1_done[t], *c_done, nxT_read.get(t - 1))
            tr = transposes("nxT_psum", bank[0], [nx[0][:, k * P:(k + 1) * P] for k in range(KD)], n, *free[0])
            nxT_read[t] = tr
            src = bank[0][:].rearrange("p (k q) -> p k q", k=KD)
            hi = copy_act("nxT_hi", nxT[r][0][:], src, tr, qkv.get(t - 2))
            lo = tt("vector", "nxT_lo", nxT[r][1][:], src, nxT[r][0][:], ALU.subtract, hi)
            free[0] = [lo]
            nxT_ready[t] = lo

        def d_qkv(t):
            r = t % 2
            for w in range(3):
                ps = products("qkv_psum", bank[1 + w][:], split_pairs([pair(nxT[r], slice(None), k) for k in range(KD)],
                                                                     [pair(Wa[w], slice(None), k) for k in range(KD)]),
                              nxT_ready[t], t_wa[2 * w], t_wa[2 * w + 1], *free[1 + w])
                qkv[t] = ps
                if w == 2:
                    v = tt("vector", "v2_done", vn[r][:], bank[3][:], absb[2][:], ALU.add, ps, t_d, *vbd_ready.get(t - 2, []))
                    free[3] = [v]
                    v2_ready[t] = v
                    continue
                x = tt("vector", "qk_done", qk[w][:], bank[1 + w][:], absb[w][:], ALU.add, ps, t_d, qkT_done.get(t - 1))
                free[1 + w] = [x]
                xe = qk[w][:].rearrange("p (c two) -> p c two", two=2)
                te = rtmp[w][:].rearrange("p (c two) -> p c two", two=2)
                se = sinb[:].rearrange("p (c two) -> p c two", two=2)
                prev = qkT_done.get(t - 1)
                m0 = tt("vector", "rope_sin", te[:, :, 0], xe[:, :, 1], se[:, :, 0], ALU.mult, x, prev)
                m1 = tt("vector", "rope_sin", te[:, :, 1], xe[:, :, 0], se[:, :, 1], ALU.mult, x, prev)
                c = tt("gpsimd", "rope_cos", qk[w][:], qk[w][:], cosb[:], ALU.mult, m1)
                rope_done[t, w] = tt("vector", "rope_done", qk[w][:], qk[w][:], rtmp[w][:], ALU.add, c)

        def d_blocks(t):
            r = t % 2
            for b2 in range(2):
                for j2 in range(2):
                    got = dma(f"vbd_loaded{r}", Vbd[r][64 * j2:64 * j2 + 64, b2, :, 64 * j2:64 * j2 + 64],
                              vn[r][64 * b2:64 * b2 + 64, :].rearrange("p (j z) -> p j z", j=4)[:, :, 64 * j2:64 * j2 + 64],
                              v2_ready[t], t_z2, pv2_done[2 * (t - 2) + 1] if t > 1 else None)
            vbd_ready[t] = [got]

        def d_turn(t):
            r = t % 2
            for w in range(2):
                tr = transposes("qkT_psum", bank[4 + w], [qk[w][:, g * P:(g + 1) * P] for g in range(4)], rope_done[t, w], *free[4 + w])
                if w == 0:
                    src = bank[4][:].rearrange("p (g b q) -> p g b q", g=4, b=2)
                    for h in range(4):
                        rs = slice(32 * h, 32 * h + 32)
                        for b2 in range(2):
                            dst = qbd2[r][rs, b2, h // 2:8:2, 64 * (h % 2):64 * (h % 2) + 64]
                            c = copy_act("qbd2_done", dst, src[rs, :, b2, :], tr, t_z2, s2_done.get(2 * (t - 2) + 1))
                    qb_ready[t] = c
                    free[4] = [c]
                else:
                    c = copy_act("kT2_done", kT2[r][:], bank[5][:].rearrange("p (g q) -> p g q", g=4), tr, s2_done.get(2 * (t - 2) + 1))
                    kt2_ready[t] = c
                    free[5] = [c]
            qkT_done[t] = tr

        def d_scores(t):
            for b2 in range(2):
                n = 2 * t + b2
                bk = bank[6 + b2]

                def emit(e, b2=b2, bk=bk):
                    for j in range(8):
                        mm = e.matmul(bk[:, j * TB:(j + 1) * TB], qbd2[t % 2][:, b2, j, :],
                                      kT2[t % 2][:, j // 2, b2 * TB:(b2 + 1) * TB], start=True, stop=True)
                    return mm
                s2_done[n] = run("tensor", "s2_psum", [qb_ready[t], kt2_ready[t], *free[6 + b2]], emit)
                sv = bk[:].rearrange("p (j k) -> p j k", j=8)
                m, s, rc = mx2[:, b2, :], sm2[:, b2, :], rc2[:, b2, :]
                wide = lambda v: v.unsqueeze(2).to_broadcast([P, 8, TB])
                pw = tr2_done.get(n - 2)
                x = run("vector", "s2_max", [s2_done[n]], lambda e, sv=sv, m=m: e.tensor_reduce(m, sv, AX, ALU.max))
                x = tt("vector", "s2_shift", P2[b2][:], sv, wide(m), ALU.subtract, x, pw)
                free[6 + b2] = [x]
                x = run("scalar", "s2_exp", [x], lambda e, b2=b2: e.activation(P2[b2][:], P2[b2][:], ACT.Exp, scale=SCALE2))
                x = run("vector", "s2_sum", [x], lambda e, b2=b2, s=s: e.tensor_reduce(s, P2[b2][:], AX, ALU.add))
                x = run("vector", "s2_sum", [x], lambda e, s=s, rc=rc: e.reciprocal(rc, s))
                p2_ready[n] = tt("vector", "p2_done", P2[b2][:], P2[b2][:], wide(rc), ALU.mult, x)

        def d_turn_p(t):
            for b2 in range(2):
                n = 2 * t + b2
                flat = P2[b2][:].rearrange("p j k -> p (j k)")
                tr2_done[n] = transposes("p2T_psum", bank[4 + b2], [flat[:, g * P:(g + 1) * P] for g in range(4)], p2_ready[n], *free[4 + b2])
                c = copy_act("p2T_done", PT2[b2][:], bank[4 + b2][:], tr2_done[n], pv2_done.get(n - 2))
                free[4 + b2] = [c]
                pt2_ready[n] = c

        def d_weigh(t):
            for b2 in range(2):
                n = 2 * t + b2
                bk = bank[1 + b2]

                def emit(e, b2=b2, bk=bk):
                    for g in range(4):
                        mm = e.matmul(bk[:, g * P:(g + 1) * P], Vbd[t % 2][:, b2, g, :], PT2[b2][:, g * P:(g + 1) * P], start=True, stop=True)
                    return mm
                pv2_done[n] = run("tensor", "o2_psum", [pt2_ready[n], *vbd_ready[t], *free[1 + b2]], emit)
                ov = bk[:].rearrange("p (g h q) -> p g h q", g=4, h=2)
                for h in range(4):
                    rs = slice(32 * h, 32 * h + 32)
                    c = copy_act("o2_copy", o2f[rs, :, b2 * TB:(b2 + 1) * TB], ov[rs, :, h % 2, :], pv2_done[n], o2_ready.get(t - 1))
                free[1 + b2] = [c]
            hi = copy_act("o2_hi", o2[0][:], o2f[:], c, out_done.get(t - 1))
            o2_ready[t] = tt("vector", "o2_lo", o2[1][:], o2f[:], o2[0][:], ALU.subtract, hi)

        def d_out(t):
            ps = products("d_psum", bank[3][:], split_pairs([pair(o2, slice(None), g) for g in range(4)],
                                                           [pair(Wa[3], slice(None), g) for g in range(4)]),
                          o2_ready[t], t_wa[6], t_wa[7], *free[3])
            out_done[t] = ps
            xb = tt("gpsimd", "x1_bias", x1[:, t, :], x1[:, t, :], absb[3][:], ALU.add, nxT_read[t], t_d)
            s = tt("vector", "x2_done", x1[:, t, :], bank[3][:], x1[:, t, :], ALU.add, ps, xb)
            free[3] = [s]
            x2_done[t] = s

        def d_norm2(t):
            n = layernorm("e_norm", x1[:, t, :], nx[1][:], 1, x2_done[t], x2T_tr.get(t - 1))
            tr = transposes("x2T_psum", bank[0], [nx[1][:, k * P:(k + 1) * P] for k in range(KD)], n, *free[0])
            x2T_tr[t] = tr
            src = bank[0][:].rearrange("p (k q) -> p k q", k=KD)
            dst = [x[:, :, t * P:(t + 1) * P] for x in x2T]
            hi = copy_act("x2T_hi", dst[0], src, tr, *c_done)
            lo = tt("vector", "x2T_lo", dst[1], src, dst[0], ALU.subtract, hi)
            free[0] = [lo]
            x2T_ready[t] = lo

        x2T_tr = {}
        wgt_done = {}
        acc_init = {}

        def route(t):
            bk = bank[0]
            ts = slice(t * P, (t + 1) * P)
            ps = products("lg_psum", bk[:, 0:E], [(x2T[i][:, k, ts].bitcast(F32), wr[:, k, :]) for i in range(2) for k in range(KD)],
                          x2T_ready[t], t_d, *free[0])
            lg, top, ex, mk, sm, ng = (rt[:, i, :] for i in range(6))
            x = tt("vector", "route", lg, bk[:, 0:E], brb[:], ALU.add, ps, t_d, wgt_done.get(t - 1))
            free[0] = [x]
            x = run("vector", "route", [x], lambda e: e.max(top, lg))
            x = run("vector", "route", [x], lambda e: e.tensor_scalar(ng[:, 0:1], top[:, 0:1], -1.0, None, ALU.mult))
            m = run("vector", "route", [x], lambda e: e.tensor_scalar(mk, lg, top[:, 1:2], None, ALU.is_ge))
            x = run("scalar", "route_exp", [x], lambda e: e.activation(ex, lg, ACT.Exp, bias=ng[:, 0:1]))
            x = tt("vector", "route", ex, ex, mk, ALU.mult, x, m)
            x = run("vector", "route", [x], lambda e: e.tensor_reduce(sm[:, 0:1], ex, AX, ALU.add))
            x = run("vector", "route", [x], lambda e: e.reciprocal(sm[:, 1:2], sm[:, 0:1]))
            wgt_done[t] = run("vector", "route", [x], lambda e: e.tensor_scalar(wgt[:, t, :], ex, sm[:, 1:2], None, ALU.mult))

        def seed(t):
            tr = run("tensor", "wT_psum", [wgt_done[t], *free[0]], lambda e: e.transpose(bank[0][0:E, 0:P], wgt[:, t, :], ident[:]))
            c = copy_act("wT_done", wT[:], bank[0][0:E, 0:P], tr, acc_mm.get(t - 1))
            ps = products("seed_psum", bank[0][:], [(wT[:], b2s[:])], c, t_d)
            acc_mm[t] = ps
            s = tt("vector", "acc_done", acc[:, t, :], bank[0][:], acc[:, t, :], ALU.add, ps)
            free[0] = [s]
            acc_init[t] = s
        acc_mm = {}

        for i in range(NT + 6):
            on = lambda k: 0 <= i - k < NT
            if on(2): d_turn(i - 2)
            if on(4): d_out(i - 4)
            if on(1): d_qkv(i - 1)
            if on(3): d_turn_p(i - 3)
            if on(0): d_norm(i)
            if on(2): d_scores(i - 2)
            if on(3): d_weigh(i - 3)
            if on(1): d_blocks(i - 1)
            if on(5): route(i - 5)
            if on(4): d_norm2(i - 4)
            if on(6): seed(i - 6)
        d_done = [acc_init[NT - 1], out_done[NT - 1], x2T_tr[NT - 1], pv2_done[2 * NT - 1], wgt_done[NT - 1], o2_ready[NT - 1]]

        w12 = a["W12"]
        w_slot = {}
        slot_read = {}

        def load_w(e, i):
            w_slot[e, i] = load_split(w12[e, i], Wh[i][0][:], Wh[i][1][:], "gpsimd", *(d_done if e == 0 else [slot_read[e - 1, i]]))

        h_free = {i: list(d_done) for i in range(4, 8)}
        y_free = {i: list(d_done) for i in range(4)}
        gl_free, hs_read, h_ready = {}, {}, {}
        steps = [(e, hb, i) for e in range(E) for hb in range(2) for i in range(NI)]
        LAG = 2

        def up(n):
            e_, hb, i = steps[n]
            bk = bank[4 + n % 4]
            cs = slice(hb * 512, hb * 512 + 512)
            ps = products("h_psum", bk[:], split_pairs([(Wh[i][0][:, k * P:(k + 1) * P], Wh[i][1][:, k * P:(k + 1) * P]) for k in range(KD)],
                                                      [pair(x2T, slice(None), k, cs) for k in range(KD)]),
                          w_slot[e_, i], *h_free[4 + n % 4])
            r = n % 2
            col = e_ * NI + i
            g = run("scalar", "gelu", [ps, h_ready.get(n - 2), t_cols, *(d_done if n < 2 else [])],
                    lambda e: e.activation(gl[r][:], bk[:], ACT.Gelu, bias=b1c[:, col:col + 1]))
            h_free[4 + n % 4] = [g]
            hi = run("vector", "h_hi", [g, hs_read.get(n - 2)], lambda e: e.tensor_copy(hs[r][0][:], gl[r][:]))
            h_ready[n] = tt("vector", "h_lo", hs[r][1][:], gl[r][:], hs[r][0][:], ALU.subtract, hi, hs_read.get(n - 2))

        def down(n):
            e_, hb, i = steps[n]
            r = n % 2

            def emit(e):
                for tt_ in range(4):
                    for m, (x, y) in enumerate(((0, 0), (0, 1), (1, 0))):
                        mm = e.matmul(bank[tt_][:], hs[r][x][:, tt_ * P:(tt_ + 1) * P], Wh[i][y][:, 512:1024],
                                      start=i == 0 and m == 0, stop=i == NI - 1 and m == 2)
                return mm
            ps = run("tensor", "y_psum", [h_ready[n], *(sum(y_free.values(), []) if i == 0 else [])], emit)
            hs_read[n] = ps
            if hb == 1:
                slot_read[e_, i] = ps
                if e_ + 1 < E:
                    load_w(e_ + 1, i)
            if i == NI - 1:
                for tt_ in range(4):
                    t = hb * 4 + tt_
                    s = run("vector", "y_done", [ps], lambda e, t=t, tt_=tt_: e.scalar_tensor_tensor(
                        acc[:, t, :], bank[tt_][:], wgt[:, t, e_:e_ + 1], acc[:, t, :], ALU.mult, ALU.add))
                    y_free[tt_] = [s]
                    if e_ == E - 1:
                        dma("out_stored", out.rearrange("(t p) d -> p t d", p=P)[:, t, :], acc[:, t, :], s)

        for i in range(NI):
            load_w(0, i)
        for n in range(len(steps) + LAG - 1):
            if n < len(steps):
                up(n)
            if n >= LAG - 1:
                down(n - LAG + 1)
        pg.close("sync", [(pg.stages["out_stored"], pg.stages["out_stored"].count)])

        pg.emit_all(stack.enter_context(nc.Block()))


def rope_tables():
    hd, dim, frame, grid = 32, 10, 256, 16
    pos = np.arange(128) % 64
    f = pos // frame
    rem = pos - frame * f
    cos = np.ones((128, hd), np.float32)
    sin = np.zeros((128, hd), np.float32)
    inv = (np.float32(1.0) / np.float32(10000.0) ** (np.arange(dim // 2, dtype=np.float32) / np.float32(dim / 2.0))).astype(np.float32)
    for axis, ids in enumerate((f, rem // grid, rem % grid)):
        freq = ids.astype(np.float32)[:, None] * inv
        cos[:, axis * dim:(axis + 1) * dim] = np.concatenate([np.cos(freq), np.cos(freq)], -1)
        sin[:, axis * dim:(axis + 1) * dim] = np.concatenate([np.sin(freq), np.sin(freq)], -1)
    sin[:, 0::2] *= -1
    return np.tile(cos, (1, 16)), np.tile(sin, (1, 16))


def kernel(**inputs):
    import concourse.bacc as bacc
    from concourse.bass_utils import run_bass_kernel_spmd

    g = {k: np.asarray(v) for k, v in inputs.items()}
    E, D, HID = g["L0_ffn_W1"].shape
    cols = lambda v: np.ascontiguousarray(v.reshape(-1, 128).T)
    cos, sin = rope_tables()
    w1 = g["L0_ffn_W1"].reshape(E, D // 128, 128, HID // 128, 128).transpose(0, 3, 2, 1, 4).reshape(E, HID // 128, 128, D)
    w2 = g["L0_ffn_W2"].reshape(E, HID // 128, 128, D)
    arrays = {
        "x": g["x"].reshape(-1, D),
        "ctxT": g["ctx_1024"].transpose(0, 2, 1).reshape(16, D // 128, 128, 512).transpose(0, 2, 1, 3),
        "Wq": g["L0_xattn_Wq"], "Wk": g["L0_xattn_Wk"], "Wv": g["L0_xattn_Wv"], "Wo": g["L0_xattn_Wo"],
        "bq": cols(g["L0_xattn_bq"]), "bk": cols(g["L0_xattn_bk"]), "bv": g["L0_xattn_bv"], "bo": g["L0_xattn_bo"],
        "gamma": g["L0_xattn_ln_gamma"], "beta": g["L0_xattn_ln_beta"],
        "aWq": g["L0_attn_Wq"], "aWk": g["L0_attn_Wk"], "aWv": g["L0_attn_Wv"], "aWo": g["L0_attn_Wo"],
        "abq": g["L0_attn_bq"], "abk": g["L0_attn_bk"], "abv": g["L0_attn_bv"], "abo": g["L0_attn_bo"],
        "W12": np.concatenate([w1, w2], -1), "b1": cols(g["L0_ffn_b1"]), "b2": g["L0_ffn_b2"],
        "Wr": g["L0_ffn_Wr"], "br": g["L0_ffn_br"],
        "cos": cos, "sin": sin, "ident": np.eye(128, dtype=np.float32),
    }
    arrays = {k: np.ascontiguousarray(v) for k, v in arrays.items()}
    nc = bacc.Bacc("TRN2", target_bir_lowering=False, num_devices=1)
    aps = {k: nc.dram_tensor(f"in_{k}", v.shape, mybir.dt.from_np(v.dtype), kind="ExternalInput").ap() for k, v in arrays.items()}
    out = nc.dram_tensor("out_x", (g["x"].shape[0] * g["x"].shape[1], D), F32, kind="ExternalOutput").ap()
    perceiver_block(nc, aps, out)
    r = run_bass_kernel_spmd(nc, [{f"in_{k}": v for k, v in arrays.items()}], core_ids=[0])
    return r.results[0]["out_x"].reshape(g["x"].shape)
```

```python
from contextlib import ExitStack

import numpy as np

import concourse.bass as bass
from concourse import mybir

F32 = mybir.dt.float32
F32R = mybir.dt.float32r
BF16 = mybir.dt.bfloat16
U32 = mybir.dt.uint32
I32 = mybir.dt.int32
ALU = mybir.AluOpType
ACT = mybir.ActivationFunctionType
AX = mybir.AxisListType.X
KB = 1024
P = 128


class Stage:

    def __init__(self, sem, step):
        self.sem, self.step, self.count = sem, step, 0

    def ticket(self):
        self.count += self.step
        return (self, self.count)


class Program:

    def __init__(self, nc, stack):
        self.nc, self.stack = nc, stack
        self.lists = {e: [] for e in ("sync", "tensor", "vector", "scalar", "gpsimd")}
        self.stages = {}
        self.optional = None
        self.skip_copies = {}

    def stage(self, name, step):
        if name not in self.stages:
            self.stages[name] = Stage(self.stack.enter_context(self.nc.semaphore(name)), step)
        return self.stages[name]

    def run(self, engine, stage, waits, emit, step=1):
        s = self.stage(stage, 16 if engine == "sync" else step)
        before = s.count
        t = s.ticket()
        item = (tuple(w for w in waits if w), emit, s)
        if self.optional is None:
            self.lists[engine].append(item)
        else:
            self.optional[1][engine].append(item)
            self.optional[2][engine].setdefault(stage, [s, before, 0])[2] += s.step
        return t

    def begin_optional(self, cond):
        self.optional = (cond, {e: [] for e in self.lists}, {e: {} for e in self.lists})

    def end_optional(self):
        cond, items, counts = self.optional
        self.optional = None
        for e in self.lists:
            if items[e]:
                self.lists[e].append((cond, items[e], list(counts[e].values())))

    def load_value(self, name, engines, ap, top, *waits):
        for e in engines:
            self.lists[e].append((tuple(waits), (name, ap, top), "value"))

    def close(self, engine, waits):
        self.lists[engine].append((tuple(waits), None, None))

    def emit_all(self, block):
        def wait(eng, reached, waits):
            for s, v in waits:
                if reached.get(id(s), 0) < v:
                    eng.wait_ge(s.sem, v)
                    reached[id(s)] = v

        def items(eng, reached, values, todo):
            for waits, fn, stage in todo:
                if callable(waits):
                    with eng.If(waits(values)):
                        items(eng, dict(reached), values, fn)
                    with eng.Else():
                        for s, before, n in stage:
                            if before:
                                eng.wait_ge(s.sem, before)
                            if s.step == 16:
                                src, dst = self.skip_copies[s]
                                eng.dma_start(dst, src).then_inc(s.sem, n)
                            else:
                                eng.sem_inc(s.sem, n)
                    continue
                wait(eng, reached, waits)
                if stage == "value":
                    name, ap, top = fn
                    values[name] = eng.value_load(ap, min_val=0, max_val=top)
                elif fn is not None:
                    fn(eng).then_inc(stage.sem, stage.step)

        def body(name):
            return lambda eng: items(eng, {}, {}, self.lists[name])

        for name, at in (("sync", block.sync), ("tensor", block.tensor), ("vector", block.vector),
                         ("scalar", block.scalar), ("gpsimd", block.gpsimd)):
            if self.lists[name]:
                at(body(name))


def perceiver_block(nc, a, out):
    B, TB, D = 16, 64, 512
    T = B * TB
    NT = T // P
    KD = D // P
    NKEY = 512
    H1, HD1 = 16, 64
    HV = H1 * HD1
    NJ = HV // P
    NKT = NKEY // P
    H2, HD2 = 16, 32
    E, HID = 8, 2048
    NI = HID // P
    EPS = 1e-5
    SCALE1 = HD1 ** -0.5
    SCALE2 = HD2 ** -0.5

    with ExitStack() as stack:
        pg = Program(nc, stack)
        run = pg.run
        base = -(-nc.sbuf_base // 64) * 64

        def place(name, kb, shape, dt=F32):
            return nc.alloc_sbuf_tensor_at(name, shape, dt, offset=base + int(kb * KB))

        bank = [stack.enter_context(nc.psum_tensor(f"bank{i}", [P, 512], F32)) for i in range(8)]

        ident = place("ident", 0, [P, P])
        b1c = place("b1c", 0.5, [P, E * NI])
        bqc = place("bqc", 1, [P, NJ])
        bqs = place("bqs", 1 + 1 / 32, [P, NJ])
        bkc = place("bkc", 1 + 2 / 32, [P, NJ])
        mv = place("mv", 1 + 3 / 32, [P, NT, 2])
        rstd = place("rstd", 1 + 5 / 32, [P, NT])
        nmr = place("nmr", 1 + 6 / 32, [P, NT])
        bst = place("bst", 1 + 7 / 32, [P, 2, 6])
        mv2 = place("mv2", 1 + 9 / 32, [P, 2, 2])
        rstd2 = place("rstd2", 1 + 10 / 32, [P, 2, 2])
        smn = place("smn", 1 + 11 / 32, [P, 3])
        ssum = place("ssum", 1 + 12 / 32, [P, 3])
        srec = place("srec", 1 + 13 / 32, [P, 3])
        mx2 = place("mx2", 1 + 14 / 32, [P, 2, 8])
        sm2 = place("sm2", 1 + 16 / 32, [P, 2, 8])
        rc2 = place("rc2", 1 + 18 / 32, [P, 2, 8])
        wgt = place("wgt", 1 + 20 / 32, [P, NT, E])
        mhalf = place("mhalf", 1 + 29 / 32, [P, 2])
        brb = place("brb", 1 + 28 / 32, [P, E])
        rt = place("rt", 2, [P, 6, E])
        wr = place("wr", 2.25, [P, KD, E])
        wT = place("wT", 2.5, [E, P])
        c0 = 3
        QO = place("QO", c0, [P, NJ, T])
        raw = [place(f"raw{i}", c0 + 96 + 4 * i, [P, 1024]) for i in range(3)]
        Wk = [place(f"Wk{i}", c0 + 32 + 16 * i, [P, KD, HV], F32R) for i in range(2)]
        Wv = [place(f"Wv{i}", c0 + 64 + 16 * i, [P, KD, HV], F32R) for i in range(2)]
        o = c0 + 108
        ctx = [[place(f"ctx{r}{i}", o + 16 * r + 8 * i, [P, KD, NKEY], F32R) for i in range(2)] for r in range(2)]
        xs = place("xs", o + 16, [P, NT, D])
        xnT = [place(f"xnT{i}", o + 32 + 16 * i, [P, KD, T], F32R) for i in range(2)]
        Wq = [place(f"Wq{i}", o + 64 + 16 * i, [P, KD, HV], F32R) for i in range(2)]
        qbd = [[place(f"qbd{r}{i}", o + 32 + 8 * r + 4 * i, [P, NJ, P], F32R) for i in range(2)] for r in range(2)]
        kT = [[place(f"kT{r}{i}", o + 48 + 4 * r + 2 * i, [P, NKEY], F32R) for i in range(2)] for r in range(2)]
        V = [place(f"V{r}", o + 56 + 8 * r, [P, NKT, 512]) for r in range(3)]
        Pr = [place(f"Pr{r}", o + 80 + 2 * r, [P, NKEY]) for r in range(2)]
        PT = [place(f"PT{r}", o + 84 + 2 * r, [P, NKEY]) for r in range(2)]
        bvb = place("bvb", o + 88, [P, HV])
        Wo = [place(f"Wo{i}", c0 + 64 + 16 * i, [P, NJ, D], F32R) for i in range(2)]
        oT = [[place(f"oT{r}{i}", o + 8 * r + 4 * i, [P, NJ, P], F32R) for i in range(2)] for r in range(2)]
        x1 = place("x1", c0 + 32, [P, NT, D])
        bob = place("bob", c0 + 48, [P, D])
        gab = place("gab", c0 + 50, [P, D])
        beb = place("beb", c0 + 52, [P, D])
        xr = [place(f"xr{r}", c0 + 54 + 2 * r, [P, D]) for r in range(2)]
        ya = [place(f"ya{r}", c0 + 58 + 2 * r, [P, D]) for r in range(2)]
        Wa = [[place(f"Wa{w}{i}", o + 16 + 16 * w + 8 * i, [P, KD, D], F32R) for i in range(2)] for w in range(4)]
        s0 = c0 + 48
        absb = [place(f"absb{w}", s0 + 2 * w, [P, D]) for w in range(4)]
        cosb = place("cosb", s0 + 8, [P, D])
        sinb = place("sinb", s0 + 10, [P, D])
        nx = [place(f"nx{r}", s0 + 12 + 2 * r, [P, D]) for r in range(2)]
        x2c = place("x2c", s0 + 30, [P, KD, P])
        nxT = [[place(f"nxT{r}{i}", s0 + 16 + 4 * r + 2 * i, [P, KD, P], F32R) for i in range(2)] for r in range(2)]
        qk = [place(f"qk{w}", s0 + 24 + 2 * w, [P, D]) for w in range(2)]
        rtmp = [place("rtmp", s0 + 28, [P, D])] * 2
        vn = [place(f"vn{r}", s0 + 32 + 2 * r, [P, D]) for r in range(2)]
        kT2 = [place(f"kT2{r}", s0 + 36 + 2 * r, [P, KD, P]) for r in range(2)]
        P2 = [place(f"P2{r}", s0 + 40 + 2 * r, [P, 8, TB]) for r in range(2)]
        PT2 = [place(f"PT2{r}", s0 + 44 + 2 * r, [P, D]) for r in range(2)]
        s1 = o
        qbd2 = [place(f"qbd2{r}", s1 + 8 * r, [P, 2, 8, P]) for r in range(2)]
        s2 = o + 80
        Vbd = [place(f"Vbd{r}", s2 + 4 * r, [P, 2, 4, P]) for r in range(2)]
        o2f = place("o2f", s2 + 8, [P, 4, P])
        o2 = [place(f"o2{i}", s2 + 10 + 2 * i, [P, 4, P], F32R) for i in range(2)]
        TW = 256
        NC = TW // P
        NW = T // TW
        xgT = [[place(f"xgT{r}{i}", c0 + 8 * r + 4 * i, [P, KD, TW], F32R) for i in range(2)] for r in range(3)]
        xg = [place(f"xg{r}", c0 + 24 + 2 * r, [P, D]) for r in range(2)]
        r0 = c0 + 28
        iota = place("iota", r0, [P, TW], BF16)
        before = place("before", r0 + 0.5, [P, P], BF16)
        ones = place("ones", r0 + 0.75, [P, P], BF16)
        rank = place("rank", r0 + 1, [P, NW, NT * E])
        rowdata = place("rowdata", r0 + 2, [P, NT, E, 6], BF16)
        rank0 = place("rank0", r0 + 2.75, [P, NT * E])
        wrest = place("wrest", r0 + 3, [P, NT, E])
        rowcol = place("rowcol", r0 + 3.25, [P, NT, 6])
        dump = place("dump", r0 + 3.5, [P, NC])
        found = place("found", r0 + 3.5 + 1 / 32, [P, NC, 6])
        rowid = place("rowid", r0 + 3.5 + 3 / 32, [P, 4, NC])
        count = place("count", r0 + 3.5 + 4 / 32, [P, E], I32)
        gidx = [place(f"gidx{r}", r0 + 3.5 + (5 + r) / 32, [P, NC], U32) for r in range(3)]
        sidx = [place(f"sidx{r}", r0 + 3.5 + (8 + r) / 32, [P, NC], U32) for r in range(3)]
        gw = [place(f"gw{r}", r0 + 3.5 + (11 + r) / 32, [P, NC]) for r in range(3)]
        maskb = place("maskb", 2.375, [P, NT, E], BF16)
        x2n_dram = nc.dram_tensor("x2n_rows", (T, D), F32).ap()
        b2s = place("b2s", s2 + 14, [E, D])
        slots = [c0 + 48 + 8 * i for i in range(6)] + [o + 8 * i for i in range(10)]
        Wh = [[place(f"Wh{s}{i}", kb + 4 * i, [P, 1024], F32R) for i in range(2)] for s, kb in enumerate(slots)]
        e0 = o + 80
        gl = [place(f"gl{r}", e0 + r, [P, TW]) for r in range(2)]
        hs = [[place(f"hs{r}{i}", e0 + 2 + 2 * r + i, [P, TW], F32R) for i in range(2)] for r in range(3)]
        ys = [place(f"ys{r}", e0 + 8 + 2 * r, [P, D]) for r in range(2)]
        onehot = place("onehot", e0 + 12, [P, NT, TW], BF16)

        def dma(stage, dst, src, *waits):
            return run("sync", stage, waits, lambda e: e.dma_start(dst, src))

        def copy_act(stage, dst, src, *waits, **kw):
            return run("scalar", stage, waits, lambda e: e.activation(dst, src, ACT.Copy, **kw))

        def tt(engine, stage, dst, x, y, op, *waits):
            return run(engine, stage, waits, lambda e: e.tensor_tensor(dst, x, y, op))

        def products(stage, dst, pairs, *waits):
            def emit(e):
                for n, (l, r) in enumerate(pairs):
                    mm = e.matmul(dst, l, r, start=n == 0, stop=n == len(pairs) - 1)
                return mm
            return run("tensor", stage, waits, emit)

        def split_pairs(lhs, rhs):
            return [p for (lh, ll), (rh, rl) in zip(lhs, rhs) for p in ((lh, rh), (lh, rl), (ll, rh))]

        def transposes(stage, dst, srcs, *waits):
            def emit(e):
                for n, s in enumerate(srcs):
                    mm = e.transpose(dst[:, n * P:(n + 1) * P], s, ident[:])
                return mm
            return run("tensor", stage, waits, emit)

        raw_used = [None] * 3
        raw_n = [0]

        def load_split(src, hi, lo, lo_engine, *waits):
            n = raw_n[0]
            raw_n[0] += 1
            r = raw[n % 3]
            shaped = r[:] if len(src.shape) == 2 else r[:].rearrange("p (a b) -> p a b", a=src.shape[1])
            got = dma(f"raw_loaded{n % 3}", shaped, src, raw_used[n % 3])
            h = copy_act("split_hi", hi, shaped, got, *waits)
            t = tt(lo_engine, f"split_lo_{lo_engine}", lo, shaped, hi, ALU.subtract, h)
            raw_used[n % 3] = t
            return t

        def layernorm(stage, src, dst, ring, *waits):
            st, m, r = bst[:, ring, :], mv2[:, ring, :], rstd2[:, ring, :]
            t = run("vector", "ln_small", waits, lambda e: e.bn_stats(st, src))
            t = run("vector", "ln_small", [t], lambda e: e.bn_aggr(m, st))
            t = run("vector", "ln_small", [t], lambda e: e.tensor_scalar(r[:, 0:1], m[:, 1:2], EPS, None, ALU.add))
            t = tt("gpsimd", "ln_pow", r[:, 0:1], r[:, 0:1], mhalf[:, 0:1], ALU.pow, t, t_mhalf)
            t = run("vector", "ln_small", [t], lambda e: e.scalar_tensor_tensor(r[:, 1:2], m[:, 0:1], -1.0, r[:, 0:1], ALU.mult, ALU.mult))
            return run("vector", stage, [t], lambda e: e.tensor_scalar(dst, src, r[:, 0:1], r[:, 1:2], ALU.mult, ALU.add))

        x_in = a["x"].rearrange("(t p) d -> p t d", p=P)
        t_mhalf = run("gpsimd", "mhalf", [], lambda e: e.memset(mhalf[:], -0.5))
        t_ident = dma("const_ident", ident[:], a["ident"])
        x_got = [dma(f"x_loaded{h}", xs[:, 2 * h:2 * h + 2, :], x_in[:, 2 * h:2 * h + 2, :]) for h in range(4)]
        for dst, name in ((bqc, "bq"), (bkc, "bk"), (b1c, "b1")):
            t_cols = dma("const_columns", dst[:], a[name])
        t_bqs = run("vector", "bq_scaled", [t_cols], lambda e: e.tensor_scalar(bqs[:], bqc[:], SCALE1, None, ALU.mult))

        t_wq = [load_split(a["Wq"][k * P:(k + 1) * P, :], Wq[0][:, k, :], Wq[1][:, k, :], "vector" if k % 2 else "gpsimd") for k in range(KD)]

        def load_ctx(b, *waits):
            for c in range(2):
                t = load_split(a["ctxT"][b, :, 2 * c:2 * c + 2, :], ctx[b % 2][0][:, 2 * c:2 * c + 2, :],
                               ctx[b % 2][1][:, 2 * c:2 * c + 2, :], "gpsimd", *waits)
            return t

        xnT_done = []
        lo_prev = [None, None]
        for h in range(4):
            for t in (2 * h, 2 * h + 1):
                st = run("vector", "x_stats", [x_got[h], pg_last if t else None],
                         lambda e, t=t: e.bn_stats(bst[:, t % 2, :], xs[:, t, :]))
                pg_last = run("vector", "x_stats", [st], lambda e, t=t: e.bn_aggr(mv[:, t, :], bst[:, t % 2, :]))
            s = slice(2 * h, 2 * h + 2)
            r = run("vector", "x_stats", [pg_last], lambda e, s=s: e.tensor_scalar(rstd[:, s], mv[:, s, 1], EPS, None, ALU.add))
            r = tt("gpsimd", "x_pow", rstd[:, s], rstd[:, s], mhalf[:], ALU.pow, r, t_mhalf)
            r = run("vector", "x_stats", [r], lambda e, s=s: e.scalar_tensor_tensor(nmr[:, s], mv[:, s, 0], -1.0, rstd[:, s], ALU.mult, ALU.mult))
            for t in (2 * h, 2 * h + 1):
                xn = run("vector", "x_normal", [r], lambda e, t=t: e.tensor_scalar(
                    xs[:, t, :], xs[:, t, :], rstd[:, t:t + 1], nmr[:, t:t + 1], ALU.mult, ALU.add))
                tr = transposes("xnT_psum", bank[t % 2], [xs[:, t, k * P:(k + 1) * P] for k in range(KD)],
                                xn, t_ident, lo_prev[t % 2])
                src = bank[t % 2][:].rearrange("p (k q) -> p k q", k=KD)
                dst = [x[:, :, t * P:(t + 1) * P] for x in xnT]
                hi = copy_act("xnT_hi", dst[0], src, tr)
                lo_prev[t % 2] = tt("vector", "xnT_lo", dst[1], src, dst[0], ALU.subtract, hi)
                xnT_done.append(lo_prev[t % 2])
        q_evac = [None, None]
        for half in range(2):
            c = slice(half * 512, half * 512 + 512)
            for j in range(NJ):
                n = half * NJ + j
                js = slice(j * P, (j + 1) * P)
                q_psum = products("q_psum", bank[2 + n % 2][:],
                                  split_pairs([(Wq[0][:, k, js], Wq[1][:, k, js]) for k in range(KD)],
                                              [(xnT[0][:, k, c], xnT[1][:, k, c]) for k in range(KD)]),
                                  *t_wq[2:], xnT_done[4 * half + 3], q_evac[n % 2])
                q_evac[n % 2] = run("scalar", "q_done", [q_psum, t_bqs], lambda e, n=n, j=j, c=c: e.activation(
                    QO[:, j, c], bank[2 + n % 2][:], ACT.Identity, bias=bqs[:, j:j + 1], scale=SCALE1))
        q_all = q_evac[1]
        a_done = q_psum

        t_ctx = {0: load_ctx(0)}
        for k in range(KD):
            t_wv = load_split(a["Wv"][k * P:(k + 1) * P, :], Wv[0][:, k, :], Wv[1][:, k, :], "gpsimd" if k % 2 else "vector")
            t_wv2 = t_wv if k == KD - 2 else (t_wv2 if k == KD - 1 else None)
        for k in range(KD):
            t_wk = load_split(a["Wk"][k * P:(k + 1) * P, :], Wk[0][:, k, :], Wk[1][:, k, :], "gpsimd" if k % 2 else "vector")
            t_wk2 = t_wk if k == KD - 2 else (t_wk2 if k == KD - 1 else None)
        w_ready = {"v": (t_wv, t_wv2), "k": (t_wk, t_wk2)}
        t_bvb = dma("const_bv", bvb[:], a["bv"].partition_broadcast(P), a_done)
        for r in range(2):
            for i in range(2):
                t_zero = run("gpsimd", "qbd_zero", [a_done], lambda e, r=r, i=i: e.memset(qbd[r][i][:].bitcast(F32), 0.0))

        NS = B * NJ
        HALF = NJ // 2
        k_free = [None, None]
        v_free = [None, None]
        s_free = [None, None]
        t_free = o_free = None
        k_ready, v_ready, p_ready, pt_ready, qbd_ready = {}, {}, {}, {}, {}
        s_done, pt_read, pv_done, tr_done, kp_done, vp_done = {}, {}, {}, {}, {}, {}
        ov = [None]

        def pair(x, *idx):
            return (x[0][idx], x[1][idx])

        def build_qbd(b):
            r = b % 2
            before = s_done.get((b - 2) * NJ + NJ - 1)
            for h in range(2):
                rows, cols = slice(64 * h, 64 * h + 64), slice(64 * h, 64 * h + 64)
                src = QO[rows, :, b * TB:(b + 1) * TB]
                hi = copy_act("qbd_hi", qbd[r][0][rows, :, cols], src, q_all, t_zero, before)
                t = tt("vector", "qbd_lo", qbd[r][1][rows, :, cols], src, qbd[r][0][rows, :, cols], ALU.subtract, hi, t_zero, before)
            qbd_ready[b] = t

        def project_v(n):
            u, kt = divmod(n, HALF)
            b, g = divmod(u, 2)
            cs = slice(g * 512, g * 512 + 512)
            ks = slice(kt * P, (kt + 1) * P)
            bk = bank[2 + n % 2]
            ps = products("v_psum", bk[:], split_pairs([pair(ctx[b % 2], slice(None), k, ks) for k in range(KD)],
                                                      [pair(Wv, slice(None), k, cs) for k in range(KD)]),
                          t_ctx[b], *w_ready["v"], v_free[n % 2])
            v_free[n % 2] = v_ready[n] = tt("vector", "v_done", V[u % 3][:, kt, :], bk[:], bvb[:, cs], ALU.add,
                                            ps, t_bvb, pv_done.get(HALF * (u - 3) + HALF - 1))
            vp_done[n] = ps

        def project_k(n):
            b, j = divmod(n, NJ)
            js = slice(j * P, (j + 1) * P)
            bk = bank[n % 2]
            ps = products("k_psum", bk[:], split_pairs([pair(Wk, slice(None), k, js) for k in range(KD)],
                                                      [pair(ctx[b % 2], slice(None), k) for k in range(KD)]),
                          t_ctx[b], *w_ready["k"], k_free[n % 2])
            dst = kT[n % 2]
            hi = run("scalar", "k_hi", [ps, t_cols, s_done.get(n - 2), a_done], lambda e: e.activation(
                dst[0][:], bk[:], ACT.Identity, bias=bkc[:, j:j + 1]))
            k_free[n % 2] = k_ready[n] = run("vector", "k_lo", [hi], lambda e: e.scalar_tensor_tensor(
                dst[1][:], bk[:], bkc[:, j:j + 1], dst[0][:], ALU.add, ALU.subtract))
            kp_done[n] = ps

        def scores(n):
            b, j = divmod(n, NJ)
            bk = bank[4 + n % 2]
            s_done[n] = products("s_psum", bk[:], split_pairs([pair(qbd[b % 2], slice(None), j)], [(kT[n % 2][0][:], kT[n % 2][1][:])]),
                                 qbd_ready[b], k_ready[n], s_free[n % 2])
            r = n % 3
            mx = run("vector", "s_max", [s_done[n], tr_done.get(n - 3)], lambda e: e.tensor_reduce(smn[:, r:r + 1], bk[:], AX, ALU.max, negate=True))
            ex = run("scalar", "s_exp", [mx, tr_done.get(n - 2), a_done], lambda e: e.activation(
                Pr[n % 2][:], bk[:], ACT.Exp, bias=smn[:, r:r + 1], accum_out=ssum[:, r:r + 1]))
            s_free[n % 2] = ex
            rc = run("vector", "s_recip", [ex], lambda e: e.reciprocal(srec[:, r:r + 1], ssum[:, r:r + 1]))
            p_ready[n] = run("vector", "p_done", [rc], lambda e: e.tensor_scalar(Pr[n % 2][:], Pr[n % 2][:], srec[:, r:r + 1], None, ALU.mult))

        def turn(n):
            nonlocal t_free
            tr_done[n] = transposes("pT_psum", bank[6], [Pr[n % 2][:, k * P:(k + 1) * P] for k in range(NKT)], p_ready[n], t_free)
            t_free = pt_ready[n] = copy_act("pT_done", PT[n % 2][:], bank[6][:], tr_done[n], pv_done.get(n - 2))

        def weigh(n):
            nonlocal o_free
            b, j = divmod(n, NJ)
            u, s = divmod(n, HALF)
            pv_done[n] = products("o_psum", bank[7][:, 0:P],
                                  [(V[u % 3][:, kt, s * P:(s + 1) * P], PT[n % 2][:, kt * P:(kt + 1) * P]) for kt in range(NKT)],
                                  pt_ready[n], v_ready[HALF * u + HALF - 1], o_free)
            for h in range(2):
                rs = slice(64 * h, 64 * h + 64)
                o_free = copy_act("o_done", QO[rs, j, b * TB:(b + 1) * TB], bank[7][rs, rs], pv_done[n], qbd_ready[b])

        build_qbd(0)
        for n in range(HALF):
            project_v(n)
        for n in range(NS + 3):
            b, j = divmod(n, NJ)
            if n < NS:
                if j == 0 and b + 1 < B:
                    t_ctx[b + 1] = load_ctx(b + 1, kp_done.get(n - 1), vp_done.get(n - 1 - HALF + HALF), a_done)
                project_k(n)
            if 0 <= n - 1 < NS:
                scores(n - 1)
            if n + HALF < NS:
                project_v(n + HALF)
            if n < NS and j == 2 and b + 1 < B:
                build_qbd(b + 1)
            if 0 <= n - 2 < NS:
                turn(n - 2)
            if 0 <= n - 3 < NS:
                weigh(n - 3)
        o_all = o_free
        k_last, v_last = kp_done[NS - 1], vp_done[NS - 1]
        b_done = pv_done[NS - 1]

        wo_in = a["Wo"].rearrange("(j p) n -> p j n", p=P)
        for c in range(4):
            t = load_split(wo_in[:, 2 * c:2 * c + 2, :], Wo[0][:, 2 * c:2 * c + 2, :], Wo[1][:, 2 * c:2 * c + 2, :],
                           "gpsimd" if c % 2 else "vector", v_last)
            t_wo2, t_wo = (t_wo, t) if c else (None, t)
        for dst, name in ((bob, "bo"), (gab, "gamma"), (beb, "beta")):
            t_cvec = dma("const_c", dst[:], a[name].partition_broadcast(P), k_last)
        t_wa = []

        def load_wa(w):
            src = a[("aWq", "aWk", "aWv", "aWo")[w]].rearrange("(k p) n -> p k n", p=P)
            for c in range(2):
                cs = slice(2 * c, 2 * c + 2)
                t_wa.append(load_split(src[:, cs, :], Wa[w][0][:, cs, :], Wa[w][1][:, cs, :], "gpsimd", b_done, k_last))

        oT_free = [None, None]
        c_free = [None, None]
        ya_free = [None, None]
        x1_done = []
        for t in range(NT):
            ts = slice(t * P, (t + 1) * P)
            r = t % 2
            got = dma(f"xr_loaded{r}", xr[r][:], x_in[:, t, :], k_last, x1_done[t - 2] if t > 1 else None)
            hi = copy_act("oT_hi", oT[r][0][:], QO[:, :, ts], o_all, oT_free[r], k_last)
            lo = tt("vector", "oT_lo", oT[r][1][:], QO[:, :, ts], oT[r][0][:], ALU.subtract, hi)
            ps = products("c_psum", bank[r][:], split_pairs([pair(oT[r], slice(None), j) for j in range(NJ)],
                                                           [pair(Wo, slice(None), j) for j in range(NJ)]),
                          lo, t_wo, t_wo2, c_free[r], k_free[r])
            oT_free[r] = ps
            y = ya[r]
            res = run("vector", "c_res", [got, ya_free[r], k_last], lambda e, t=t, r=r, y=y: e.tensor_scalar(
                y[:], xr[r][:], rstd[:, t:t + 1], nmr[:, t:t + 1], ALU.mult, ALU.add))
            res = tt("gpsimd", "c_bias", y[:], y[:], bob[:], ALU.add, res, t_cvec)
            s = tt("vector", "c_sum", y[:], bank[r][:], y[:], ALU.add, res, ps)
            c_free[r] = s
            s = layernorm("c_norm", y[:], y[:], r, s)
            s = tt("gpsimd", "c_gamma", y[:], y[:], gab[:], ALU.mult, s)
            s = tt("gpsimd", "c_beta", y[:], y[:], beb[:], ALU.add, s)
            s = tt("vector", "x1_done", x1[:, t, :], y[:], xr[r][:], ALU.add, s, k_last)
            ya_free[r] = s
            x1_done.append(s)
            if t % 2 == 0:
                load_wa(t // 2)
        c_done = [x1_done[-1], ps]

        for w in range(4):
            t_d = dma("const_d", absb[w][:], a[("abq", "abk", "abv", "abo")[w]].partition_broadcast(P), *c_done)
        t_d = dma("const_d", cosb[:], a["cos"], *c_done)
        t_d = dma("const_d", sinb[:], a["sin"], *c_done)
        t_d = dma("const_d", brb[:], a["br"].partition_broadcast(P))
        t_d = dma("const_d", wr[:], a["Wr"].rearrange("(k p) e -> p k e", p=P))
        t_d = dma("const_d", b2s[:], a["b2"], b_done)
        for dst, name in ((iota, "iota"), (before, "before"), (ones, "ones"), (rowcol, "rowcol"), (dump, "dump")):
            t_route = dma("const_route", dst[:], a[name], *c_done)
        for r in range(2):
            t_z2 = run("gpsimd", "d_zero", c_done, lambda e, r=r: e.memset(qbd2[r][:], 0.0))
            t_z2 = run("gpsimd", "d_zero", c_done + [b_done], lambda e, r=r: e.memset(Vbd[r][:], 0.0))

        nxT_ready, qkv, rope_done, qb_ready, kt2_ready, vbd_ready = {}, {}, {}, {}, {}, {}
        s2_done, p2_ready, pt2_done, o2_ready, x2_done, nxT_read, q3_done = {}, {}, {}, {}, {}, {}, {}
        bank0 = list(c_done)
        free = {i: list(c_done) for i in range(8)}
        tr2_done, pv2_done, out_done, lg_done, qk_read, qkT_done = {}, {}, {}, {}, {}, {}
        pt2_ready, x2T_ready, v2_ready = {}, {}, {}
        acc = x1

        def d_norm(t):
            r = t % 2
            n = layernorm("d_norm", x1[:, t, :], nx[0][:], 0, x1_done[t], *c_done, nxT_read.get(t - 1))
            tr = transposes("nxT_psum", bank[0], [nx[0][:, k * P:(k + 1) * P] for k in range(KD)], n, *free[0])
            nxT_read[t] = tr
            src = bank[0][:].rearrange("p (k q) -> p k q", k=KD)
            hi = copy_act("nxT_hi", nxT[r][0][:], src, tr, qkv.get(t - 2))
            lo = tt("vector", "nxT_lo", nxT[r][1][:], src, nxT[r][0][:], ALU.subtract, hi)
            free[0] = [lo]
            nxT_ready[t] = lo

        def d_qkv(t):
            r = t % 2
            for w in range(3):
                ps = products("qkv_psum", bank[1 + w][:], split_pairs([pair(nxT[r], slice(None), k) for k in range(KD)],
                                                                     [pair(Wa[w], slice(None), k) for k in range(KD)]),
                              nxT_ready[t], t_wa[2 * w], t_wa[2 * w + 1], *free[1 + w])
                qkv[t] = ps
                if w == 2:
                    v = tt("vector", "v2_done", vn[r][:], bank[3][:], absb[2][:], ALU.add, ps, t_d, *vbd_ready.get(t - 2, []))
                    free[3] = [v]
                    v2_ready[t] = v
                    continue
                x = tt("vector", "qk_done", qk[w][:], bank[1 + w][:], absb[w][:], ALU.add, ps, t_d, qkT_done.get(t - 1))
                free[1 + w] = [x]
                xe = qk[w][:].rearrange("p (c two) -> p c two", two=2)
                te = rtmp[w][:].rearrange("p (c two) -> p c two", two=2)
                se = sinb[:].rearrange("p (c two) -> p c two", two=2)
                prev = qkT_done.get(t - 1) if w == 0 else rope_done[t, 0]
                m0 = tt("vector", "rope_sin", te[:, :, 0], xe[:, :, 1], se[:, :, 0], ALU.mult, x, prev)
                m1 = tt("vector", "rope_sin", te[:, :, 1], xe[:, :, 0], se[:, :, 1], ALU.mult, x, prev)
                c = tt("gpsimd", "rope_cos", qk[w][:], qk[w][:], cosb[:], ALU.mult, m1)
                rope_done[t, w] = tt("vector", "rope_done", qk[w][:], qk[w][:], rtmp[w][:], ALU.add, c)

        def d_blocks(t):
            r = t % 2
            for b2 in range(2):
                for j2 in range(2):
                    got = dma(f"vbd_loaded{r}", Vbd[r][64 * j2:64 * j2 + 64, b2, :, 64 * j2:64 * j2 + 64],
                              vn[r][64 * b2:64 * b2 + 64, :].rearrange("p (j z) -> p j z", j=4)[:, :, 64 * j2:64 * j2 + 64],
                              v2_ready[t], t_z2, pv2_done[2 * (t - 2) + 1] if t > 1 else None)
            vbd_ready[t] = [got]

        def d_turn(t):
            r = t % 2
            for w in range(2):
                tr = transposes("qkT_psum", bank[4 + w], [qk[w][:, g * P:(g + 1) * P] for g in range(4)], rope_done[t, w], *free[4 + w])
                if w == 0:
                    src = bank[4][:].rearrange("p (g b q) -> p g b q", g=4, b=2)
                    for h in range(4):
                        rs = slice(32 * h, 32 * h + 32)
                        for b2 in range(2):
                            dst = qbd2[r][rs, b2, h // 2:8:2, 64 * (h % 2):64 * (h % 2) + 64]
                            c = copy_act("qbd2_done", dst, src[rs, :, b2, :], tr, t_z2, s2_done.get(2 * (t - 2) + 1))
                    qb_ready[t] = c
                    free[4] = [c]
                else:
                    c = copy_act("kT2_done", kT2[r][:], bank[5][:].rearrange("p (g q) -> p g q", g=4), tr, s2_done.get(2 * (t - 2) + 1))
                    kt2_ready[t] = c
                    free[5] = [c]
            qkT_done[t] = tr

        def d_scores(t):
            for b2 in range(2):
                n = 2 * t + b2
                bk = bank[6 + b2]

                def emit(e, b2=b2, bk=bk):
                    for j in range(8):
                        mm = e.matmul(bk[:, j * TB:(j + 1) * TB], qbd2[t % 2][:, b2, j, :],
                                      kT2[t % 2][:, j // 2, b2 * TB:(b2 + 1) * TB], start=True, stop=True)
                    return mm
                s2_done[n] = run("tensor", "s2_psum", [qb_ready[t], kt2_ready[t], *free[6 + b2]], emit)
                sv = bk[:].rearrange("p (j k) -> p j k", j=8)
                m, s, rc = mx2[:, b2, :], sm2[:, b2, :], rc2[:, b2, :]
                wide = lambda v: v.unsqueeze(2).to_broadcast([P, 8, TB])
                pw = tr2_done.get(n - 2)
                x = run("vector", "s2_max", [s2_done[n]], lambda e, sv=sv, m=m: e.tensor_reduce(m, sv, AX, ALU.max))
                x = tt("vector", "s2_shift", P2[b2][:], sv, wide(m), ALU.subtract, x, pw)
                free[6 + b2] = [x]
                x = run("scalar", "s2_exp", [x], lambda e, b2=b2: e.activation(P2[b2][:], P2[b2][:], ACT.Exp, scale=SCALE2))
                x = run("vector", "s2_sum", [x], lambda e, b2=b2, s=s: e.tensor_reduce(s, P2[b2][:], AX, ALU.add))
                x = run("vector", "s2_sum", [x], lambda e, s=s, rc=rc: e.reciprocal(rc, s))
                p2_ready[n] = tt("vector", "p2_done", P2[b2][:], P2[b2][:], wide(rc), ALU.mult, x)

        def d_turn_p(t):
            for b2 in range(2):
                n = 2 * t + b2
                flat = P2[b2][:].rearrange("p j k -> p (j k)")
                tr2_done[n] = transposes("p2T_psum", bank[4 + b2], [flat[:, g * P:(g + 1) * P] for g in range(4)], p2_ready[n], *free[4 + b2])
                c = copy_act("p2T_done", PT2[b2][:], bank[4 + b2][:], tr2_done[n], pv2_done.get(n - 2))
                free[4 + b2] = [c]
                pt2_ready[n] = c

        def d_weigh(t):
            for b2 in range(2):
                n = 2 * t + b2
                bk = bank[1 + b2]

                def emit(e, b2=b2, bk=bk):
                    for g in range(4):
                        mm = e.matmul(bk[:, g * P:(g + 1) * P], Vbd[t % 2][:, b2, g, :], PT2[b2][:, g * P:(g + 1) * P], start=True, stop=True)
                    return mm
                pv2_done[n] = run("tensor", "o2_psum", [pt2_ready[n], *vbd_ready[t], *free[1 + b2]], emit)
                ov = bk[:].rearrange("p (g h q) -> p g h q", g=4, h=2)
                for h in range(4):
                    rs = slice(32 * h, 32 * h + 32)
                    c = copy_act("o2_copy", o2f[rs, :, b2 * TB:(b2 + 1) * TB], ov[rs, :, h % 2, :], pv2_done[n], o2_ready.get(t - 1))
                free[1 + b2] = [c]
            hi = copy_act("o2_hi", o2[0][:], o2f[:], c, out_done.get(t - 1))
            o2_ready[t] = tt("vector", "o2_lo", o2[1][:], o2f[:], o2[0][:], ALU.subtract, hi)

        def d_out(t):
            ps = products("d_psum", bank[3][:], split_pairs([pair(o2, slice(None), g) for g in range(4)],
                                                           [pair(Wa[3], slice(None), g) for g in range(4)]),
                          o2_ready[t], t_wa[6], t_wa[7], *free[3])
            out_done[t] = ps
            xb = tt("gpsimd", "x1_bias", x1[:, t, :], x1[:, t, :], absb[3][:], ALU.add, nxT_read[t], t_d)
            s = tt("vector", "x2_done", x1[:, t, :], bank[3][:], x1[:, t, :], ALU.add, ps, xb)
            free[3] = [s]
            x2_done[t] = s

        def d_norm2(t):
            n = layernorm("e_norm", x1[:, t, :], nx[1][:], 1, x2_done[t], x2T_tr.get(t - 1), x2n_stored.get(t - 1))
            x2n_stored[t] = dma("x2n_stored", x2n_dram[t * P:(t + 1) * P, :], nx[1][:], n)
            tr = transposes("x2T_psum", bank[0], [nx[1][:, k * P:(k + 1) * P] for k in range(KD)], n, *free[0])
            x2T_tr[t] = tr
            src = bank[0][:].rearrange("p (k q) -> p k q", k=KD)
            x2T_ready[t] = copy_act("x2T_done", x2c[:], src, tr, lg_done.get(t - 1))
            free[0] = [x2T_ready[t]]

        x2n_stored = {}
        x2T_tr = {}
        wgt_done = {}
        acc_init = {}

        def route(t):
            bk = bank[0]
            ts = slice(t * P, (t + 1) * P)
            ps = products("lg_psum", bk[:, 0:E], [(x2c[:, k, :], wr[:, k, :]) for k in range(KD)], x2T_ready[t], t_d, *free[0])
            lg_done[t] = ps
            lg, top, ex, mk, sm, ng = (rt[:, i, :] for i in range(6))
            x = tt("vector", "route", lg, bk[:, 0:E], brb[:], ALU.add, ps, t_d, wgt_done.get(t - 1))
            free[0] = [x]
            x = run("vector", "route", [x], lambda e: e.max(top, lg))
            x = run("vector", "route", [x], lambda e: e.tensor_scalar(ng[:, 0:1], top[:, 0:1], -1.0, None, ALU.mult))
            m = run("vector", "route", [x], lambda e: e.tensor_scalar(mk, lg, top[:, 1:2], None, ALU.is_ge))
            m = run("vector", "route", [m], lambda e: e.tensor_copy(maskb[:, t, :], mk))
            x = run("scalar", "route_exp", [x], lambda e: e.activation(ex, lg, ACT.Exp, bias=ng[:, 0:1]))
            x = tt("vector", "route", ex, ex, mk, ALU.mult, x, m)
            x = run("vector", "route", [x], lambda e: e.tensor_reduce(sm[:, 0:1], ex, AX, ALU.add))
            x = run("vector", "route", [x], lambda e: e.reciprocal(sm[:, 1:2], sm[:, 0:1]))
            wgt_done[t] = run("vector", "route", [x], lambda e: e.tensor_scalar(wgt[:, t, :], ex, sm[:, 1:2], None, ALU.mult))

        def seed(t):
            tr = run("tensor", "wT_psum", [wgt_done[t], *free[0]], lambda e: e.transpose(bank[0][0:E, 0:P], wgt[:, t, :], ident[:]))
            c = copy_act("wT_done", wT[:], bank[0][0:E, 0:P], tr, acc_mm.get(t - 1))
            ps = products("seed_psum", bank[0][:], [(wT[:], b2s[:])], c, t_d)
            acc_mm[t] = ps
            s = tt("vector", "acc_done", acc[:, t, :], bank[0][:], acc[:, t, :], ALU.add, ps)
            free[0] = [s]
            acc_init[t] = s
            t_out = dma("out_seeded", out[t * P:(t + 1) * P, :], acc[:, t, :], s)
            if t < NC:
                t_out = dma("out_seeded", out[T + t * P:T + (t + 1) * P, :], acc[:, t, :], s)
            out_seeded[0] = t_out
        acc_mm, out_seeded = {}, [None]

        for i in range(NT + 6):
            on = lambda k: 0 <= i - k < NT
            if on(2): d_turn(i - 2)
            if on(4): d_out(i - 4)
            if on(1): d_qkv(i - 1)
            if on(3): d_turn_p(i - 3)
            if on(0): d_norm(i)
            if on(2): d_scores(i - 2)
            if on(3): d_weigh(i - 3)
            if on(1): d_blocks(i - 1)
            if on(5): route(i - 5)
            if on(4): d_norm2(i - 4)
            if on(6): seed(i - 6)
        d_done = [acc_init[NT - 1], out_done[NT - 1], x2T_tr[NT - 1], pv2_done[2 * NT - 1], wgt_done[NT - 1], o2_ready[NT - 1]]

        def emit_rank(e):
            for t in range(NT):
                for u in range(t + 1):
                    e.matmul(bank[0][:, t * E:(t + 1) * E], (before if u == t else ones)[:], maskb[:, u, :], start=u == 0, stop=u == t)
            for u in range(NT):
                mm = e.matmul(bank[0][:, NT * E:(NT + 1) * E], ones[:], maskb[:, u, :], start=u == 0, stop=u == NT - 1)
            return mm
        rk = run("tensor", "rank_psum", [wgt_done[NT - 1], t_route, *free[0]], emit_rank)
        flat_mask = maskb[:].rearrange("p t e -> p (t e)")
        x = run("vector", "rank_done", [rk], lambda e: e.scalar_tensor_tensor(rank0[:], bank[0][:, 0:NT * E], 1.0, flat_mask, ALU.add, ALU.mult))
        t_count = run("vector", "rank_done", [rk], lambda e: e.tensor_copy(count[:], bank[0][:, NT * E:(NT + 1) * E]))
        for k in range(NW):
            t_rank = run("vector", "rank_done", [x], lambda e, k=k: e.tensor_scalar(rank[:, k, :], rank0[:], -1.0 - k * TW, None, ALU.add))
        x = run("vector", "rowdata", [t_route], lambda e: e.tensor_copy(rowdata[:], rowcol[:].unsqueeze(2).to_broadcast([P, NT, E, 6])))
        rest = wgt
        for k in range(3):
            x = run("vector", "rowdata", [x, *wgt_done.values()], lambda e, k=k, rest=rest: e.tensor_copy(rowdata[:, :, :, 2 + k], rest[:]))
            if k < 2:
                x = tt("vector", "rowdata", wrest[:], rest[:], rowdata[:, :, :, 2 + k], ALU.subtract, x)
                rest = wrest
        t_rowdata = x

        w12 = a["W12"]
        w_slot, slot_read = {}, {}

        def load_w(e, i):
            w_slot[e, i] = load_split(w12[e, i], Wh[i][0][:], Wh[i][1][:], "vector" if i % 3 == 2 else "gpsimd",
                                      *(d_done if e == 0 else [slot_read[e - 1, i]]))

        h_free = {i: [*d_done, t_rank, t_count] for i in range(3)}
        y_free = {c: list(d_done) for c in range(NC)}
        found_free, xt_free = [list(d_done)], {c: list(d_done) for c in range(NC)}
        xgT_read, xgT_ready, idx_ready, gathered, xg_read, ys_stored, scattered = {}, {}, {}, {}, {}, {}, [None]
        onehot_ready, onehot_read = [None], [None]
        state = {"h": 0, "g_last": {}, "hs_last": {}, "hs_read": {}}

        def buffer_of(e, k):
            return e % 2 if k == 0 else 2

        def find_a(e_, k):
            for t in range(NT):
                col = t * E + e_
                x = run("vector", "onehot", [t_rank, onehot_read[0], *(d_done if onehot_read[0] is None else [])],
                        lambda e, t=t, col=col: e.tensor_scalar(onehot[:, t, :], iota[:], rank[:, k, col:col + 1], None, ALU.is_equal))
            onehot_ready[0] = x

        def find_b(e_, k):
            r = buffer_of(e_, k)

            def emit(e):
                for c in range(NC):
                    for t in range(NT):
                        mm = e.matmul(bank[5][:, 8 * c:8 * c + 6], onehot[:, t, c * P:(c + 1) * P], rowdata[:, t, e_, :],
                                      start=t == 0, stop=t == NT - 1)
                return mm
            ps = run("tensor", "found_psum", [onehot_ready[0], t_rowdata, *found_free[0]], emit)
            onehot_read[0] = ps
            x = run("vector", "found", [ps], lambda e: e.tensor_copy(found[:], bank[5][:, 0:8 * NC].rearrange("p (c z) -> p c z", c=NC)[:, :, 0:6]))
            found_free[0] = [x]
            f = lambda z: found[:, :, z]
            old = [gathered.get(r), scattered[0]]
            row = run("vector", "found", [x], lambda e: e.scalar_tensor_tensor(rowid[:, 0, :], f(0), float(P), f(1), ALU.mult, ALU.add))
            w = tt("vector", "found", rowid[:, 1, :], f(2), f(3), ALU.add, x)
            u = tt("vector", "found", rowid[:, 2, :], f(5), dump[:], ALU.mult, x)
            g = run("vector", "found", [row, *old], lambda e: e.tensor_copy(gidx[r][:], rowid[:, 0, :]))
            v = tt("vector", "found", rowid[:, 3, :], rowid[:, 0, :], dump[:], ALU.add, row)
            w = tt("vector", "found", gw[r][:], rowid[:, 1, :], f(4), ALU.add, w, *ys_stored.values())
            v = tt("vector", "found", sidx[r][:], rowid[:, 3, :], rowid[:, 2, :], ALU.subtract, v, u, *old)
            idx_ready[e_, k] = v
            for c in range(NC):
                gathered[r] = run("gpsimd", "gathered", [g, *x2n_stored.values(), xg_read.get(c)],
                                  lambda e, c=c: e.indirect_dma_start(xg[c][:], None, x2n_dram, bass.IndirectOffsetOnAxis(gidx[r][:, c:c + 1], 0)), step=16)
            gathered[e_, k] = gathered[r]

        def find_c(e_, k):
            r = buffer_of(e_, k)
            for c in range(NC):
                tr = transposes("xgT_psum", bank[6 + c], [xg[c][:, q * P:(q + 1) * P] for q in range(KD)], gathered[e_, k], *xt_free[c])
                xg_read[c] = tr
                src = bank[6 + c][:].rearrange("p (k q) -> p k q", k=KD)
                dst = [z[:, :, c * P:(c + 1) * P] for z in xgT[r]]
                hi = copy_act("xgT_hi", dst[0], src, tr, xgT_read.get(r), *(d_done if e_ == 0 else []))
                lo = tt("vector", "xgT_lo", dst[1], src, dst[0], ALU.subtract, hi)
                xt_free[c] = [lo]
            xgT_ready[e_, k] = lo

        def up(e_, k, i):
            r = buffer_of(e_, k)
            n = state["h"]
            state["h"] += 1
            bk = bank[n % 3]
            ps = products("h_psum", bk[:, 0:TW], split_pairs([(Wh[i][0][:, q * P:(q + 1) * P], Wh[i][1][:, q * P:(q + 1) * P]) for q in range(KD)],
                                                            [pair(xgT[r], slice(None), q) for q in range(KD)]),
                          w_slot[e_, i], xgT_ready[e_, k], *h_free[n % 3])
            xgT_read[r] = ps
            col = e_ * NI + i
            g = run("scalar", "gelu", [ps, state["g_last"].get(n % 2), t_cols, *(d_done if n < 2 else [])],
                    lambda e: e.activation(gl[n % 2][:], bk[:, 0:TW], ACT.Gelu, bias=b1c[:, col:col + 1]))
            h_free[n % 3] = [g]
            hi = run("vector", "h_hi", [g, state["hs_read"].get(n % 3), *(d_done if n < 3 else [])],
                     lambda e: e.tensor_copy(hs[n % 3][0][:], gl[n % 2][:]))
            lo = tt("vector", "h_lo", hs[n % 3][1][:], gl[n % 2][:], hs[n % 3][0][:], ALU.subtract, hi)
            state["g_last"][n % 2] = state["hs_last"][n % 3] = lo
            return n

        def down(e_, k, i, n):
            r = buffer_of(e_, k)
            hr = hs[n % 3]

            def emit(e):
                for c in range(NC):
                    for m, (x, y) in enumerate(((0, 0), (0, 1), (1, 0))):
                        mm = e.matmul(bank[3 + c][:], hr[x][:, c * P:(c + 1) * P], Wh[i][y][:, 512:1024],
                                      start=i == 0 and m == 0, stop=i == NI - 1 and m == 2)
                return mm
            ps = run("tensor", "y_psum", [state["hs_last"][n % 3], *(sum(y_free.values(), []) if i == 0 else [])], emit)
            state["hs_read"][n % 3] = ps
            slot_read[e_, i] = ps
            if i == NI - 1:
                last = scattered[0]
                for c in range(NC):
                    s = run("scalar", "y_done", [ps, idx_ready[e_, k], ys_stored.get(c), *(d_done if e_ == 0 else [])],
                            lambda e, c=c: e.activation(ys[c][:], bank[3 + c][:], ACT.Copy, scale=gw[r][:, c:c + 1]))
                    y_free[c] = [s]
                    scattered[0] = run("gpsimd", "out_added", [s, last, out_seeded[0]], lambda e, c=c: e.indirect_dma_start(
                        out, bass.IndirectOffsetOnAxis(sidx[r][:, c:c + 1], 0), ys[c][:], None, compute_op=ALU.add), step=16)
                for c in range(NC):
                    ys_stored[c] = scattered[0]

        def expert_tile(e_, k, between):
            ns = {}
            for i in range(NI + 1):
                if i < NI:
                    ns[i] = up(e_, k, i)
                if i >= 1:
                    down(e_, k, i - 1, ns[i - 1])
                    if k == 0 and e_ + 1 < E:
                        load_w(e_ + 1, i - 1)
                for fn in between.get(i, ()):
                    fn()

        for i in range(3):
            load_w(0, i)
        for k in (0, 1):
            find_a(0, k)
            find_b(0, k)
            find_c(0, k)
        for i in range(3, NI):
            load_w(0, i)
        skipped = nc.dram_tensor("skipped", (2, P, 8), F32).ap()
        for n, name in enumerate(("gathered", "out_added")):
            pg.skip_copies[pg.stage(name, 16)] = (ident[:, 0:8], skipped[n])
        pg.close("gpsimd", [t_ident])
        for e_ in range(E):
            pg.load_value("rows", ("tensor", "vector", "scalar", "gpsimd"), count[0:1, e_:e_ + 1], T, t_count)
            pg.begin_optional(lambda v: v["rows"] > TW)
            expert_tile(e_, 1, {})
            pg.end_optional()
            pg.begin_optional(lambda v: v["rows"] > 2 * TW)
            for k in range(2, NW):
                find_a(e_, k)
                find_b(e_, k)
                find_c(e_, k)
                expert_tile(e_, k, {})
            pg.end_optional()
            if e_ + 1 < E:
                n_ = e_ + 1
                expert_tile(e_, 0, {1: [lambda: find_a(n_, 0)], 3: [lambda: find_b(n_, 0)], 6: [lambda: find_c(n_, 0)],
                                    8: [lambda: find_a(n_, 1)], 10: [lambda: find_b(n_, 1)], 13: [lambda: find_c(n_, 1)]})
            else:
                expert_tile(e_, 0, {})
        pg.close("gpsimd", [scattered[0]])

        pg.emit_all(stack.enter_context(nc.Block()))


def rope_tables():
    hd, dim, frame, grid = 32, 10, 256, 16
    pos = np.arange(128) % 64
    f = pos // frame
    rem = pos - frame * f
    cos = np.ones((128, hd), np.float32)
    sin = np.zeros((128, hd), np.float32)
    inv = (np.float32(1.0) / np.float32(10000.0) ** (np.arange(dim // 2, dtype=np.float32) / np.float32(dim / 2.0))).astype(np.float32)
    for axis, ids in enumerate((f, rem // grid, rem % grid)):
        freq = ids.astype(np.float32)[:, None] * inv
        cos[:, axis * dim:(axis + 1) * dim] = np.concatenate([np.cos(freq), np.cos(freq)], -1)
        sin[:, axis * dim:(axis + 1) * dim] = np.concatenate([np.sin(freq), np.sin(freq)], -1)
    sin[:, 0::2] *= -1
    return np.tile(cos, (1, 16)), np.tile(sin, (1, 16))


def routing_tables():

    bf16 = mybir.dt.np(BF16)
    rowcol = np.zeros((128, 8, 6), np.float32)
    rowcol[:, :, 0] = np.arange(8)
    rowcol[:, :, 1] = np.arange(128)[:, None]
    rowcol[:, :, 5] = 1
    return {
        "iota": np.broadcast_to(np.arange(256), (128, 256)).astype(bf16),
        "before": np.triu(np.ones((128, 128)), 1).astype(bf16),
        "ones": np.ones((128, 128), bf16),
        "rowcol": rowcol,
        "dump": (1024 + np.arange(2)[None, :] * 128 + np.arange(128)[:, None]).astype(np.float32),
    }


def kernel(**inputs):
    import concourse.bacc as bacc
    from concourse.bass_utils import run_bass_kernel_spmd

    g = {k: np.asarray(v) for k, v in inputs.items()}
    E, D, HID = g["L0_ffn_W1"].shape
    cols = lambda v: np.ascontiguousarray(v.reshape(-1, 128).T)
    cos, sin = rope_tables()
    w1 = g["L0_ffn_W1"].reshape(E, D // 128, 128, HID // 128, 128).transpose(0, 3, 2, 1, 4).reshape(E, HID // 128, 128, D)
    w2 = g["L0_ffn_W2"].reshape(E, HID // 128, 128, D)
    arrays = {
        "x": g["x"].reshape(-1, D),
        "ctxT": g["ctx_1024"].transpose(0, 2, 1).reshape(16, D // 128, 128, 512).transpose(0, 2, 1, 3),
        "Wq": g["L0_xattn_Wq"], "Wk": g["L0_xattn_Wk"], "Wv": g["L0_xattn_Wv"], "Wo": g["L0_xattn_Wo"],
        "bq": cols(g["L0_xattn_bq"]), "bk": cols(g["L0_xattn_bk"]), "bv": g["L0_xattn_bv"], "bo": g["L0_xattn_bo"],
        "gamma": g["L0_xattn_ln_gamma"], "beta": g["L0_xattn_ln_beta"],
        "aWq": g["L0_attn_Wq"], "aWk": g["L0_attn_Wk"], "aWv": g["L0_attn_Wv"], "aWo": g["L0_attn_Wo"],
        "abq": g["L0_attn_bq"], "abk": g["L0_attn_bk"], "abv": g["L0_attn_bv"], "abo": g["L0_attn_bo"],
        "W12": np.concatenate([w1, w2], -1), "b1": cols(g["L0_ffn_b1"]), "b2": g["L0_ffn_b2"],
        "Wr": g["L0_ffn_Wr"], "br": g["L0_ffn_br"],
        "cos": cos, "sin": sin, "ident": np.eye(128, dtype=np.float32),
        **routing_tables(),
    }
    arrays = {k: np.ascontiguousarray(v) for k, v in arrays.items()}
    nc = bacc.Bacc("TRN2", target_bir_lowering=False, num_devices=1)
    aps = {k: nc.dram_tensor(f"in_{k}", v.shape, mybir.dt.from_np(v.dtype), kind="ExternalInput").ap() for k, v in arrays.items()}
    rows = g["x"].shape[0] * g["x"].shape[1]
    out = nc.dram_tensor("out_x", (rows + 256, D), F32, kind="ExternalOutput").ap()
    perceiver_block(nc, aps, out)
    r = run_bass_kernel_spmd(nc, [{f"in_{k}": v for k, v in arrays.items()}], core_ids=[0])
    return r.results[0]["out_x"][:rows].reshape(g["x"].shape)
```

```python
from contextlib import ExitStack

import numpy as np

import concourse.bass as bass
from concourse import mybir

F32 = mybir.dt.float32
F32R = mybir.dt.float32r
BF16 = mybir.dt.bfloat16
U32 = mybir.dt.uint32
I32 = mybir.dt.int32
ALU = mybir.AluOpType
ACT = mybir.ActivationFunctionType
AX = mybir.AxisListType.X
KB = 1024
P = 128


class Stage:

    def __init__(self, sem, step):
        self.sem, self.step, self.count = sem, step, 0

    def ticket(self):
        self.count += self.step
        return (self, self.count)


class Program:

    def __init__(self, nc, stack):
        self.nc, self.stack = nc, stack
        self.lists = {e: [] for e in ("sync", "tensor", "vector", "scalar", "gpsimd")}
        self.stages = {}
        self.optional = None
        self.skip_copies = {}

    def stage(self, name, step):
        if name not in self.stages:
            self.stages[name] = Stage(self.stack.enter_context(self.nc.semaphore(name)), step)
        return self.stages[name]

    def run(self, engine, stage, waits, emit, step=1):
        if isinstance(stage, tuple):
            assert self.optional is None
            stages = tuple(self.stage(x, step) for x in stage)
            self.lists[engine].append((tuple(w for w in waits if w), emit, stages))
            return tuple(x.ticket() for x in stages)
        s = self.stage(stage, 16 if engine == "sync" else step)
        before = s.count
        t = s.ticket()
        item = (tuple(w for w in waits if w), emit, s)
        if self.optional is None:
            self.lists[engine].append(item)
        else:
            self.optional[1][engine].append(item)
            self.optional[2][engine].setdefault(stage, [s, before, 0])[2] += s.step
        return t

    def begin_optional(self, cond):
        self.optional = (cond, {e: [] for e in self.lists}, {e: {} for e in self.lists})

    def end_optional(self):
        cond, items, counts = self.optional
        self.optional = None
        for e in self.lists:
            if items[e]:
                self.lists[e].append((cond, items[e], list(counts[e].values())))

    def load_value(self, name, engines, ap, top, *waits):
        for e in engines:
            self.lists[e].append((tuple(waits), (name, ap, top), "value"))

    def close(self, engine, waits):
        self.lists[engine].append((tuple(waits), None, None))

    def emit_all(self, block):
        def wait(eng, reached, waits):
            for s, v in waits:
                if reached.get(id(s), 0) < v:
                    eng.wait_ge(s.sem, v)
                    reached[id(s)] = v

        def items(eng, reached, values, todo):
            for waits, fn, stage in todo:
                if callable(waits):
                    with eng.If(waits(values)):
                        items(eng, dict(reached), values, fn)
                    with eng.Else():
                        for s, before, n in stage:
                            if before:
                                eng.wait_ge(s.sem, before)
                            if s.step == 16:
                                src, dst = self.skip_copies[s]
                                eng.dma_start(dst, src).then_inc(s.sem, n)
                            else:
                                eng.sem_inc(s.sem, n)
                    continue
                wait(eng, reached, waits)
                if stage == "value":
                    name, ap, top = fn
                    values[name] = eng.value_load(ap, min_val=0, max_val=top)
                elif isinstance(stage, tuple):
                    for s, ins in zip(stage, fn(eng)):
                        ins.then_inc(s.sem, s.step)
                elif fn is not None:
                    fn(eng).then_inc(stage.sem, stage.step)

        def body(name):
            return lambda eng: items(eng, {}, {}, self.lists[name])

        for name, at in (("sync", block.sync), ("tensor", block.tensor), ("vector", block.vector),
                         ("scalar", block.scalar), ("gpsimd", block.gpsimd)):
            if self.lists[name]:
                at(body(name))


def perceiver_block(nc, a, out):
    B, TB, D = 16, 64, 512
    T = B * TB
    NT = T // P
    KD = D // P
    NKEY = 512
    H1, HD1 = 16, 64
    HV = H1 * HD1
    NJ = HV // P
    NKT = NKEY // P
    H2, HD2 = 16, 32
    E, HID = 8, 2048
    NI = HID // P
    EPS = 1e-5
    SCALE1 = HD1 ** -0.5
    SCALE2 = HD2 ** -0.5

    with ExitStack() as stack:
        pg = Program(nc, stack)
        run = pg.run
        base = -(-nc.sbuf_base // 64) * 64

        def place(name, kb, shape, dt=F32):
            return nc.alloc_sbuf_tensor_at(name, shape, dt, offset=base + int(kb * KB))

        psum = stack.enter_context(nc.psum_tensor("psum", [P, 8, 512], F32))
        bank = [psum[:, i, :] for i in range(8)]

        small_at = [0]

        def small(name, shape, dt=F32):
            kb = small_at[0]
            n = int(np.prod(shape[1:])) * (2 if dt == BF16 else 4)
            small_at[0] += -(-n // 32) / 32
            assert small_at[0] <= 3
            return place(name, kb, shape, dt)

        ident = small("ident", [P, P])
        b1c = small("b1c", [P, E * NI])
        wT = small("wT", [E, P])
        bqc = small("bqc", [P, NJ])
        bqs = small("bqs", [P, NJ])
        bkc = small("bkc", [P, NJ])
        mv = small("mv", [P, NT, 2])
        rstd = small("rstd", [P, NT])
        nmr = small("nmr", [P, NT])
        bst = small("bst", [P, 4, 6])
        mv2 = small("mv2", [P, 4, 2])
        rstd2 = small("rstd2", [P, 4, 2])
        mhalf = small("mhalf", [P, 2])
        smn, ssum, srec = (small(n, [P, 3]) for n in ("smn", "ssum", "srec"))
        mx2, sm2, rc2 = (small(n, [P, 2, 8]) for n in ("mx2", "sm2", "rc2"))
        wgt = small("wgt", [P, NT, E])
        brb = small("brb", [P, E])
        rt = small("rt", [P, 6, E])
        maskb = small("maskb", [P, NT, E], BF16)
        maskc = small("maskc", [P, NT, E], BF16)
        c0 = 3
        QO = place("QO", c0, [P, NJ, T])
        raw = [place(f"raw{i}", c0 + (96 if i < 3 else 20) + 4 * i, [P, 1024]) for i in range(6)]
        Wk = [place(f"Wk{i}", c0 + 32 + 16 * i, [P, KD, HV], F32R) for i in range(2)]
        Wv = [place(f"Wv{i}", c0 + 64 + 16 * i, [P, KD, HV], F32R) for i in range(2)]
        o = c0 + 108
        ctx = [[place(f"ctx{r}{i}", o + 16 * r + 8 * i, [P, KD, NKEY], F32R) for i in range(2)] for r in range(2)]
        xs = place("xs", o + 16, [P, NT, D])
        xnT = [place(f"xnT{i}", o + 32 + 16 * i, [P, KD, T], F32R) for i in range(2)]
        Wq = [place(f"Wq{i}", o + 64 + 16 * i, [P, KD, HV], F32R) for i in range(2)]
        qbd = [[place(f"qbd{r}{i}", o + 32 + 8 * r + 4 * i, [P, NJ, P], F32R) for i in range(2)] for r in range(2)]
        kT = [[place(f"kT{r}{i}", o + 48 + 4 * r + 2 * i, [P, NKEY], F32R) for i in range(2)] for r in range(2)]
        V = [place(f"V{r}", o + 56 + 8 * r, [P, NKT, 512]) for r in range(3)]
        Pr = [place(f"Pr{r}", o + 80 + 2 * r, [P, NKEY]) for r in range(2)]
        PT = [place(f"PT{r}", o + 84 + 2 * r, [P, NKEY]) for r in range(2)]
        bvb = place("bvb", o + 88, [P, HV])
        Wo = [place(f"Wo{i}", c0 + 64 + 16 * i, [P, NJ, D], F32R) for i in range(2)]
        oT = [[place(f"oT{r}{i}", o + 8 * r + 4 * i, [P, NJ, P], F32R) for i in range(2)] for r in range(2)]
        x1 = place("x1", c0 + 32, [P, NT, D])
        bob = place("bob", c0 + 48, [P, D])
        gab = place("gab", c0 + 50, [P, D])
        beb = place("beb", c0 + 52, [P, D])
        xr = [place(f"xr{r}", c0 + 54 + 2 * r, [P, D]) for r in range(2)]
        ya = [place(f"ya{r}", c0 + 58 + 2 * r, [P, D]) for r in range(2)]
        nxc = place("nxc", c0 + 62, [P, D])
        nxall = place("nxall", c0, [P, 2 * KD, T], F32R)
        Wa = [[place(f"Wa{w}{i}", o + 16 + 16 * w + 8 * i, [P, KD, D], F32R) for i in range(2)] for w in range(4)]
        s0 = c0 + 48
        absb = [place(f"absb{w}", s0 + 2 * w, [P, D]) for w in range(4)]
        cosb = place("cosb", s0 + 8, [P, D])
        sinb = place("sinb", s0 + 10, [P, D])
        nx2 = place("nx2", s0 + 12, [P, D])
        wrp = place("wrp", s0 + 14, [P, KD, P])
        r0 = s0 + 16
        x2c = place("x2c", s0 + 20, [P, KD, P])
        qk = [place(f"qk{w}", s0 + 22 + 2 * w, [P, D]) for w in range(2)]
        rtmp = [place(f"rtmp{w}", s0 + 26 + 2 * w, [P, D]) for w in range(2)]
        vn = [place(f"vn{r}", s0 + 30 + 2 * r, [P, D]) for r in range(2)]
        kT2 = [place(f"kT2{r}", s0 + 34 + 2 * r, [P, KD, P]) for r in range(2)]
        P2 = [place(f"P2{r}", s0 + 38 + 2 * r, [P, 8, TB]) for r in range(2)]
        PT2 = [place(f"PT2{r}", s0 + 42 + 2 * r, [P, D]) for r in range(2)]
        s1 = o
        qbd2 = [place(f"qbd2{r}", s1 + 8 * r, [P, 2, 8, P]) for r in range(2)]
        s2 = o + 80
        Vbd = [place(f"Vbd{r}", s2 + 4 * r, [P, 2, 4, P]) for r in range(2)]
        o2f = place("o2f", s2 + 8, [P, 4, P])
        o2 = [place(f"o2{i}", s2 + 10 + 2 * i, [P, 4, P], F32R) for i in range(2)]
        TW = 256
        NC = TW // P
        NW = T // TW
        xgT = [[place(f"xgT{r}{i}", c0 + 8 * r + 4 * i, [P, KD, TW], F32R) for i in range(2)] for r in range(3)]
        xg = [place(f"xg{r}", c0 + (24 if r < 2 else 40) + 2 * r, [P, D]) for r in range(4)]
        iota = place("iota", r0, [P, TW], BF16)
        before = place("before", r0 + 0.5, [P, P], BF16)
        ones = place("ones", r0 + 0.75, [P, P], BF16)
        rank = place("rank", r0 + 1, [P, NW, NT * E])
        rowdata = place("rowdata", r0 + 2, [P, NT, E, 6], BF16)
        rank0 = place("rank0", r0 + 2.75, [P, NT * E])
        wrest = place("wrest", r0 + 3, [P, NT, E])
        rowcol = place("rowcol", r0 + 3.25, [P, NT, 6])
        dump = place("dump", r0 + 3.5, [P, NC])
        found = place("found", r0 + 3.5 + 1 / 32, [P, NC, 6])
        rowid = place("rowid", r0 + 3.5 + 3 / 32, [P, 4, NC])
        count = place("count", r0 + 3.5 + 4 / 32, [P, E], I32)
        gidx = [place(f"gidx{r}", r0 + 3.5 + (5 + r) / 32, [P, NC], U32) for r in range(3)]
        sidx = [place(f"sidx{r}", r0 + 3.5 + (8 + r) / 32, [P, NC], U32) for r in range(3)]
        gw = [place(f"gw{r}", r0 + 3.5 + (11 + r) / 32, [P, NC]) for r in range(3)]
        x2n_dram = nc.dram_tensor("x2n_rows", (T, D), F32).ap()
        b2s = place("b2s", s2 + 14, [E, D])
        slots = [(kb, kb + 4) for kb in ([o + 16 + 8 * i for i in range(6)] + [o, o + 8, s0, s0 + 28, s0 + 36])]
        slots.append((s0 + 44, c0 + 28))
        slots += [(kb, kb + 4) for kb in (o + 64, o + 72, s0 + 8, s0 + 20)]
        Wh = [[place(f"Wh{n}{i}", kb[i], [P, 1024], F32R) for i in range(2)] for n, kb in enumerate(slots)]
        e0 = o + 80
        gl = [place(f"gl{r}", e0 + r, [P, TW]) for r in range(2)]
        hs = [[place(f"hs{r}{i}", e0 + 2 + 2 * r + i, [P, TW], F32R) for i in range(2)] for r in range(3)]
        ys = [place(f"ys{r}", e0 + 8 + 2 * r, [P, D]) for r in range(2)]
        onehot = place("onehot", e0 + 12, [P, NT, TW], BF16)

        def dma(stage, dst, src, *waits):
            return run("sync", stage, waits, lambda e: e.dma_start(dst, src))

        def copy_act(stage, dst, src, *waits, **kw):
            return run("scalar", stage, waits, lambda e: e.activation(dst, src, ACT.Copy, **kw))

        def tt(engine, stage, dst, x, y, op, *waits):
            return run(engine, stage, waits, lambda e: e.tensor_tensor(dst, x, y, op))

        def products(stage, dst, pairs, *waits):
            def emit(e):
                for n, (l, r) in enumerate(pairs):
                    mm = e.matmul(dst, l, r, start=n == 0, stop=n == len(pairs) - 1)
                return mm
            return run("tensor", stage, waits, emit)

        def split_pairs(lhs, rhs):
            return [p for (lh, ll), (rh, rl) in zip(lhs, rhs) for p in ((lh, rh), (lh, rl), (ll, rh))]

        def transposes(stage, dst, srcs, *waits):
            def emit(e):
                for n, s in enumerate(srcs):
                    mm = e.transpose(dst[:, n * P:(n + 1) * P], s, ident[:])
                return mm
            return run("tensor", stage, waits, emit)

        raw_used = [None] * 6
        ring = {"next": 0, "size": 3}

        def load_split(src, hi, lo, lo_engine, *waits):
            n = ring["next"]
            ring["next"] = (n + 1) % ring["size"]
            r = raw[n]
            shaped = r[:] if len(src.shape) == 2 else r[:].rearrange("p (a b) -> p a b", a=src.shape[1])
            got = dma(f"raw_loaded{n}", shaped, src, raw_used[n])
            h = copy_act("split_hi", hi, shaped, got, *waits)
            t = tt(lo_engine, f"split_lo_{lo_engine}", lo, shaped, hi, ALU.subtract, h)
            raw_used[n] = t
            return t

        def ln_stats(src, ring, *waits):
            st, m, r = bst[:, ring, :], mv2[:, ring, :], rstd2[:, ring, :]
            t = run("vector", "ln_small", [*waits, ln_used.get(ring)], lambda e: e.bn_stats(st, src))
            t = run("vector", "ln_small", [t], lambda e: e.bn_aggr(m, st))
            t = run("vector", "ln_small", [t], lambda e: e.tensor_scalar(r[:, 0:1], m[:, 1:2], EPS, None, ALU.add))
            return tt("gpsimd", "ln_pow", r[:, 0:1], r[:, 0:1], mhalf[:, 0:1], ALU.pow, t, t_mhalf)

        ln_used = {}

        def ln_apply(stage, src, dst, ring, *waits):
            m, r = mv2[:, ring, :], rstd2[:, ring, :]
            t = run("vector", "ln_small", waits, lambda e: e.scalar_tensor_tensor(r[:, 1:2], m[:, 0:1], -1.0, r[:, 0:1], ALU.mult, ALU.mult))
            t = run("scalar", stage, [t], lambda e: e.activation(dst, src, ACT.Identity, bias=r[:, 1:2], scale=r[:, 0:1]))
            ln_used[ring] = t
            return t

        x_in = a["x"].rearrange("(t p) d -> p t d", p=P)
        t_mhalf = run("gpsimd", "mhalf", [], lambda e: e.memset(mhalf[:], -0.5))
        t_ident = dma("const_ident", ident[:], a["ident"])
        x_got = [dma(f"x_loaded{h}", xs[:, 2 * h:2 * h + 2, :], x_in[:, 2 * h:2 * h + 2, :]) for h in range(4)]
        for dst, name in ((bqc, "bq"), (bkc, "bk"), (b1c, "b1")):
            t_cols = dma("const_columns", dst[:], a[name])
        t_bqs = run("vector", "bq_scaled", [t_cols], lambda e: e.tensor_scalar(bqs[:], bqc[:], SCALE1, None, ALU.mult))

        t_wq = [load_split(a["Wq"][k * P:(k + 1) * P, :], Wq[0][:, k, :], Wq[1][:, k, :], "vector" if k % 2 else "gpsimd") for k in range(KD)]

        def load_ctx(b, *waits):
            for c in range(2):
                t = load_split(a["ctxT"][b, :, 2 * c:2 * c + 2, :], ctx[b % 2][0][:, 2 * c:2 * c + 2, :],
                               ctx[b % 2][1][:, 2 * c:2 * c + 2, :], "gpsimd", *waits)
            return t

        xnT_done, xn_done, bank_read = {}, {}, {}

        def x_stats(h):
            for t in (2 * h, 2 * h + 1):
                x = run("vector", "x_stats", [x_got[h], stats_last[0]], lambda e, t=t: e.bn_stats(bst[:, t % 4, :], xs[:, t, :]))
                stats_last[0] = run("vector", "x_stats", [x], lambda e, t=t: e.bn_aggr(mv[:, t, :], bst[:, t % 4, :]))
            s = slice(2 * h, 2 * h + 2)
            r = run("vector", "x_stats", [stats_last[0]], lambda e: e.tensor_scalar(rstd[:, s], mv[:, s, 1], EPS, None, ALU.add))
            pow_done[h] = tt("gpsimd", "x_pow", rstd[:, s], rstd[:, s], mhalf[:], ALU.pow, r, t_mhalf)

        stats_last, pow_done = [None], {}

        def x_normal(h):
            s = slice(2 * h, 2 * h + 2)
            r = run("vector", "x_stats", [pow_done[h]], lambda e: e.scalar_tensor_tensor(nmr[:, s], mv[:, s, 0], -1.0, rstd[:, s], ALU.mult, ALU.mult))
            for t in (2 * h, 2 * h + 1):
                xn_done[t] = run("vector", "x_normal", [r], lambda e, t=t: e.tensor_scalar(
                    xs[:, t, :], xs[:, t, :], rstd[:, t:t + 1], nmr[:, t:t + 1], ALU.mult, ALU.add))

        def x_turn(t):
            tr = transposes("xnT_psum", bank[t % 2], [xs[:, t, k * P:(k + 1) * P] for k in range(KD)],
                            xn_done[t], t_ident, bank_read.get(t % 2))
            src = bank[t % 2].rearrange("p (k q) -> p k q", k=KD)
            dst = [x[:, :, t * P:(t + 1) * P] for x in xnT]
            hi = copy_act("xnT_hi", dst[0], src, tr)
            bank_read[t % 2] = xnT_done[t] = tt("vector", "xnT_lo", dst[1], src, dst[0], ALU.subtract, hi)

        q_evac = [None, None]

        def project_q(half, j):
            c = slice(half * 512, half * 512 + 512)
            n = half * NJ + j
            js = slice(j * P, (j + 1) * P)
            ps = products("q_psum", bank[2 + n % 2],
                          split_pairs([(Wq[0][:, k, js], Wq[1][:, k, js]) for k in range(KD)],
                                      [(xnT[0][:, k, c], xnT[1][:, k, c]) for k in range(KD)]),
                          *t_wq[2:], xnT_done[4 * half + 3], q_evac[n % 2])
            q_evac[n % 2] = run("scalar", "q_done", [ps, t_bqs], lambda e: e.activation(
                QO[:, j, c], bank[2 + n % 2], ACT.Identity, bias=bqs[:, j:j + 1], scale=SCALE1))
            return ps

        x_stats(0)
        for h in range(2):
            x_stats(h + 1)
            x_normal(h)
            x_turn(2 * h)
            x_turn(2 * h + 1)
        loads = [lambda: t_ctx.update({0: load_ctx(0)})]
        for w, src in (("v", "Wv"), ("k", "Wk")):
            for k in range(KD):
                loads.append(lambda w=w, src=src, k=k: w_ready[w].append(load_split(
                    a[src][k * P:(k + 1) * P, :], *[x[:, k, :] for x in (Wv if w == "v" else Wk)], "gpsimd" if k % 2 else "vector")))
        t_ctx, w_ready = {}, {"v": [], "k": []}
        for half in range(2):
            for j in range(NJ):
                if half == 0 and j in (1, 3):
                    h = 2 + j // 2
                    if h < 3:
                        x_stats(h + 1)
                    x_normal(h)
                    x_turn(2 * h)
                    x_turn(2 * h + 1)
                q_psum = project_q(half, j)
                if loads:
                    loads.pop(0)()
        q_all = q_evac[1]
        a_done = q_psum
        t_bvb = dma("const_bv", bvb[:], a["bv"].partition_broadcast(P), a_done)
        for r in range(2):
            for i in range(2):
                t_zero = run("vector", "qbd_zero", [a_done], lambda e, r=r, i=i: e.memset(qbd[r][i][:].bitcast(F32), 0.0))

        NS = B * NJ
        HALF = NJ // 2
        k_free = [bank_read[0], bank_read[1]]
        v_free = list(q_evac)
        s_free = [None, None]
        t_free = o_free = None
        k_ready, v_ready, p_ready, pt_ready, qbd_ready = {}, {}, {}, {}, {}
        o_done = {}
        s_done, pt_read, pv_done, tr_done, kp_done, vp_done = {}, {}, {}, {}, {}, {}
        ov = [None]

        def pair(x, *idx):
            return (x[0][idx], x[1][idx])

        def build_qbd(b):
            r = b % 2
            before = s_done.get((b - 2) * NJ + NJ - 1)
            for h in range(2):
                rows, cols = slice(64 * h, 64 * h + 64), slice(64 * h, 64 * h + 64)
                src = QO[rows, :, b * TB:(b + 1) * TB]
                hi = copy_act("qbd_hi", qbd[r][0][rows, :, cols], src, q_all, t_zero, before)
                t = tt("vector", "qbd_lo", qbd[r][1][rows, :, cols], src, qbd[r][0][rows, :, cols], ALU.subtract, hi, t_zero, before)
            qbd_ready[b] = t

        def project_v(n):
            u, kt = divmod(n, HALF)
            b, g = divmod(u, 2)
            cs = slice(g * 512, g * 512 + 512)
            ks = slice(kt * P, (kt + 1) * P)
            bk = bank[2 + n % 2]
            ps = products("v_psum", bk, split_pairs([pair(ctx[b % 2], slice(None), k, ks) for k in range(KD)],
                                                      [pair(Wv, slice(None), k, cs) for k in range(KD)]),
                          t_ctx[b], *w_ready["v"], v_free[n % 2])
            v_free[n % 2] = v_ready[n] = tt("vector", "v_done", V[u % 3][:, kt, :], bk[:], bvb[:, cs], ALU.add,
                                            ps, t_bvb, pv_done.get(HALF * (u - 3) + HALF - 1))
            vp_done[n] = ps

        def project_k(n):
            b, j = divmod(n, NJ)
            js = slice(j * P, (j + 1) * P)
            bk = bank[n % 2]
            ps = products("k_psum", bk[:], split_pairs([pair(Wk, slice(None), k, js) for k in range(KD)],
                                                      [pair(ctx[b % 2], slice(None), k) for k in range(KD)]),
                          t_ctx[b], *w_ready["k"], k_free[n % 2])
            dst = kT[n % 2]
            hi = run("scalar", "k_hi", [ps, t_cols, s_done.get(n - 2), a_done], lambda e: e.activation(
                dst[0][:], bk[:], ACT.Identity, bias=bkc[:, j:j + 1]))
            k_free[n % 2] = k_ready[n] = run("vector", "k_lo", [hi], lambda e: e.scalar_tensor_tensor(
                dst[1][:], bk[:], bkc[:, j:j + 1], dst[0][:], ALU.add, ALU.subtract))
            kp_done[n] = ps

        def scores(n):
            b, j = divmod(n, NJ)
            bk = bank[4 + n % 2]
            s_done[n] = products("s_psum", bk[:], split_pairs([pair(qbd[b % 2], slice(None), j)], [(kT[n % 2][0][:], kT[n % 2][1][:])]),
                                 qbd_ready[b], k_ready[n], s_free[n % 2])
            r = n % 3
            mx = run("vector", "s_max", [s_done[n], tr_done.get(n - 3)], lambda e: e.tensor_reduce(smn[:, r:r + 1], bk[:], AX, ALU.max, negate=True))
            ex = run("scalar", "s_exp", [mx, tr_done.get(n - 2), a_done], lambda e: e.activation(
                Pr[n % 2][:], bk[:], ACT.Exp, bias=smn[:, r:r + 1], accum_out=ssum[:, r:r + 1]))
            s_free[n % 2] = ex
            rc = run("vector", "s_recip", [ex], lambda e: e.reciprocal(srec[:, r:r + 1], ssum[:, r:r + 1]))
            p_ready[n] = run("vector", "p_done", [rc], lambda e: e.tensor_scalar(Pr[n % 2][:], Pr[n % 2][:], srec[:, r:r + 1], None, ALU.mult))

        def turn(n):
            nonlocal t_free
            tr_done[n] = transposes("pT_psum", bank[6], [Pr[n % 2][:, k * P:(k + 1) * P] for k in range(NKT)], p_ready[n], t_free)
            t_free = pt_ready[n] = copy_act("pT_done", PT[n % 2][:], bank[6][:], tr_done[n], pv_done.get(n - 2))

        def weigh(n):
            nonlocal o_free
            b, j = divmod(n, NJ)
            u, s = divmod(n, HALF)
            pv_done[n] = products("o_psum", bank[7][:, 0:P],
                                  [(V[u % 3][:, kt, s * P:(s + 1) * P], PT[n % 2][:, kt * P:(kt + 1) * P]) for kt in range(NKT)],
                                  pt_ready[n], v_ready[HALF * u + HALF - 1], o_free)
            for h in range(2):
                rs = slice(64 * h, 64 * h + 64)
                o_free = copy_act("o_done", QO[rs, j, b * TB:(b + 1) * TB], bank[7][rs, rs], pv_done[n], qbd_ready[b])
            o_done[n] = o_free

        t_wo = []
        wo_in = a["Wo"].rearrange("(j p) n -> p j n", p=P)
        build_qbd(0)
        for n in range(HALF):
            project_v(n)
        for n in range(NS + 3):
            b, j = divmod(n, NJ)
            if n < NS:
                if j == 0 and b + 1 < B:
                    t_ctx[b + 1] = load_ctx(b + 1, kp_done.get(n - 1), vp_done.get(n - 1 - HALF + HALF), a_done)
                project_k(n)
            if 0 <= n - 1 < NS:
                scores(n - 1)
            if n + HALF < NS:
                project_v(n + HALF)
            if n < NS and j == 2 and b + 1 < B:
                build_qbd(b + 1)
            if 0 <= n - 2 < NS:
                turn(n - 2)
            if 0 <= n - 3 < NS:
                weigh(n - 3)
            if n >= NS - HALF + 1 and len(t_wo) < 4:
                c = len(t_wo)
                t_wo.append(load_split(wo_in[:, 2 * c:2 * c + 2, :], Wo[0][:, 2 * c:2 * c + 2, :], Wo[1][:, 2 * c:2 * c + 2, :],
                                       "gpsimd" if c % 2 else "vector", vp_done[NS - 1]))
        o_all = o_free
        k_last, v_last = kp_done[NS - 1], vp_done[NS - 1]
        b_done = pv_done[NS - 1]

        for dst, name in ((bob, "bo"), (gab, "gamma"), (beb, "beta")):
            t_cvec = dma("const_c", dst[:], a[name].partition_broadcast(P), k_last)
        t_wa = []

        def load_wa(n):
            w, c = divmod(n, 2)
            src = a[("aWq", "aWk", "aWv", "aWo")[w]].rearrange("(k p) n -> p k n", p=P)
            cs = slice(2 * c, 2 * c + 2)
            t_wa.append(load_split(src[:, cs, :], Wa[w][0][:, cs, :], Wa[w][1][:, cs, :], "gpsimd", b_done, k_last))

        oT_done, oT_read, c_read, ya_read, ya_pre, x1_pre, x1_done = {}, {}, {}, {}, {}, {}, {}
        xr_got, c_psum, nxc_read, nx_done = {}, {}, {}, {}
        ctx0_free = [kp_done[NS - NJ - 1], vp_done[NS - NJ - 1]]

        def c_split(t):
            r, ts = t % 2, slice(t * P, (t + 1) * P)
            hi = copy_act("oT_hi", oT[r][0][:], QO[:, :, ts], o_done[2 * NJ * (t + 1) - 1], oT_read.get(t - 2), *ctx0_free)
            oT_done[t] = tt("vector", "oT_lo", oT[r][1][:], QO[:, :, ts], oT[r][0][:], ALU.subtract, hi)

        def c_before(t):
            r = t % 2
            xr_got[t] = dma(f"xr_loaded{r}", xr[r][:], x_in[:, t, :], k_last, ya_pre.get(t - 2), x1_pre.get(t - 2))
            x = run("scalar", "c_res", [xr_got[t], ya_read.get(t - 2), k_last], lambda e: e.activation(
                ya[r][:], xr[r][:], ACT.Identity, bias=nmr[:, t:t + 1], scale=rstd[:, t:t + 1]))
            ya_pre[t] = tt("gpsimd", "c_bias", ya[r][:], ya[r][:], bob[:], ALU.add, x, t_cvec)
            x1_pre[t] = tt("gpsimd", "c_beta", x1[:, t, :], xr[r][:], beb[:], ALU.add, xr_got[t], t_cvec)

        def c_product(t):
            r = t % 2
            c_psum[t] = products("c_psum", bank[r], split_pairs([pair(oT[r], slice(None), j) for j in range(NJ)],
                                                               [pair(Wo, slice(None), j) for j in range(NJ)]),
                                 oT_done[t], *t_wo, c_read.get(t - 2), k_free[r])
            oT_read[t] = c_psum[t]

        ya_stat, x1_stat = {}, {}

        def c_sum(t):
            r = t % 2
            c_read[t] = tt("vector", "c_sum", ya[r][:], bank[r], ya[r][:], ALU.add, ya_pre[t], c_psum[t])
            ya_stat[t] = ln_stats(ya[r][:], r, c_read[t])

        def c_scale(t):
            r = t % 2
            y = run("vector", "c_norm", [c_read[t], ya_stat[t]], lambda e: e.scalar_tensor_tensor(
                ya[r][:], ya[r][:], mv2[:, r, 0:1], gab[:], ALU.subtract, ALU.mult))
            x1_done[t] = ya_read[t] = ln_used[r] = run("vector", "x1_done", [y, x1_pre[t]], lambda e: e.scalar_tensor_tensor(
                x1[:, t, :], ya[r][:], rstd2[:, r, 0:1], x1[:, t, :], ALU.mult, ALU.add))
            x1_stat[t] = ln_stats(x1[:, t, :], 2 + r, x1_done[t])

        def c_normal(t):
            r, ts = t % 2, slice(t * P, (t + 1) * P)
            n = ln_apply("nx_done", x1[:, t, :], nxc[:], 2 + r, x1_stat[t], nxc_read.get(t - 1))
            tr = transposes("nxT_psum", bank[2 + r], [nxc[:, k * P:(k + 1) * P] for k in range(KD)], n, nx_done.get(t - 2), v_free[r])
            nxc_read[t] = tr
            src = bank[2 + r].rearrange("p (k q) -> p k q", k=KD)
            nx_hi[t] = copy_act("nxT_hi", nxall[:, 0:KD, ts], src, tr, oT_done[t])

        nx_hi = {}

        def c_normal_lo(t):
            src, ts = bank[2 + t % 2].rearrange("p (k q) -> p k q", k=KD), slice(t * P, (t + 1) * P)
            nx_done[t] = tt("vector", "nxT_lo", nxall[:, KD:2 * KD, ts], src, nxall[:, 0:KD, ts], ALU.subtract, nx_hi[t])

        c_split(0)
        c_before(0)
        for t in range(NT + 3):
            if t + 1 < NT:
                c_split(t + 1)
            if t < NT:
                c_product(t)
                load_wa(t)
            if 0 <= t - 2 < NT:
                c_normal(t - 2)
            if 0 <= t - 1 < NT:
                c_scale(t - 1)
            if 0 <= t - 2 < NT:
                c_normal_lo(t - 2)
            if t + 1 < NT:
                c_before(t + 1)
            if t < NT:
                c_sum(t)
        c_done = [x1_done[NT - 1], c_psum[NT - 1], nxc_read[NT - 1], nx_done[NT - 1]]

        c_end = [x1_done[NT - 1], c_psum[NT - 1], nxc_read[NT - 1]]
        for w in range(4):
            t_d = dma("const_d", absb[w][:], a[("abq", "abk", "abv", "abo")[w]].partition_broadcast(P), *c_end)
        t_d = dma("const_d", cosb[:], a["cos"], *c_end)
        t_d = dma("const_d", sinb[:], a["sin"], *c_end)
        for r in range(2):
            t_z2 = run("gpsimd", "d_zero", c_end, lambda e, r=r: e.memset(qbd2[r][:], 0.0))
        for r in range(2):
            t_z2 = run("gpsimd", "d_zero", c_end + [b_done], lambda e, r=r: e.memset(Vbd[r][:], 0.0))
        t_zw = run("gpsimd", "d_zero", c_end, lambda e: e.memset(wrp[:], 0.0))
        t_e = dma("const_e", brb[:], a["br"].partition_broadcast(P))
        t_e = dma("const_e", wrp[:, :, 0:E], a["Wr"].rearrange("(k p) e -> p k e", p=P), t_zw)
        t_e = dma("const_e", b2s[:], a["b2"], b_done)
        for dst, name in ((iota, "iota"), (before, "before"), (ones, "ones"), (rowcol, "rowcol"), (dump, "dump")):
            t_e = dma("const_e", dst[:], a[name], *c_end)

        free = {i: list(c_done) for i in range(8)}
        qkv_psum, rope_done, v2_ready, vbd_ready, qb_ready, kt2_ready, qk_read = {}, {}, {}, {}, {}, {}, {}
        s2_psum, p2_ready, p2_read, pt2_ready, o2_psum, o2_ready, o2_read, x2_done = {}, {}, {}, {}, {}, {}, {}, {}
        o2f_read = {}
        acc = x1

        def qkv_pairs(t, w):
            ts = slice(t * P, (t + 1) * P)
            return split_pairs([(nxall[:, k, ts], nxall[:, KD + k, ts]) for k in range(KD)], [pair(Wa[w], slice(None), k) for k in range(KD)])

        def score_pairs(t, b2):
            r = t % 2
            return [(bank[5 + b2][:, j * TB:(j + 1) * TB], qbd2[r][:, b2, j, :], kT2[r][:, j // 2, b2 * TB:(b2 + 1) * TB]) for j in range(8)]

        def d_products(w, t, ts):
            big = qkv_pairs(t, w) if t is not None else []
            narrow = score_pairs(ts, w) if ts is not None else []

            def emit(e):
                last = [None, None]
                for n in range(max(len(big), len(narrow))):
                    if n < len(big):
                        last[0] = e.matmul(bank[w], *big[n], start=n == 0, stop=n == len(big) - 1)
                    if n < len(narrow):
                        last[1] = e.matmul(*narrow[n], start=True, stop=True)
                return tuple(x for x in last if x is not None)
            stages = (["qkv_psum"] if big else []) + (["s2_psum"] if narrow else [])
            waits = []
            if big:
                waits += [nx_done[t], *t_wa[2 * w:2 * w + 2], *free[w]]
            if narrow:
                waits += [qb_ready[ts], kt2_ready[ts], *free[5 + w]]
            got = dict(zip(stages, run("tensor", tuple(stages), waits, emit)))
            if big:
                qkv_psum[t, w] = got["qkv_psum"]
            if narrow:
                s2_psum[ts, w] = got["s2_psum"]

        def wide(v):
            return v.unsqueeze(2).to_broadcast([P, 8, TB])

        def d_softmax_a(t, b2):
            sv = bank[5 + b2].rearrange("p (j k) -> p j k", j=8)
            m = mx2[:, b2, :]
            x = run("vector", "s2_max", [s2_psum[t, b2]], lambda e: e.tensor_reduce(m, sv, AX, ALU.max))
            x = tt("vector", "s2_shift", P2[b2][:], sv, wide(m), ALU.subtract, x, p2_read.get(b2))
            free[5 + b2] = [x]
            p2_ready[t, b2] = run("scalar", "s2_exp", [x], lambda e: e.activation(P2[b2][:], P2[b2][:], ACT.Exp, scale=SCALE2))

        def d_softmax_b(t, b2):
            s, rc = sm2[:, b2, :], rc2[:, b2, :]
            x = run("vector", "s2_sum", [p2_ready[t, b2]], lambda e: e.tensor_reduce(s, P2[b2][:], AX, ALU.add))
            x = run("vector", "s2_sum", [x], lambda e: e.reciprocal(rc, s))
            p2_ready[t, b2] = tt("vector", "p2_done", P2[b2][:], P2[b2][:], wide(rc), ALU.mult, x)

        x1_bias = {}

        def d_bias(t, w):
            x = tt("vector", "qk_done", qk[w][:], bank[w], absb[w][:], ALU.add, qkv_psum[t, w], t_d, qk_read.get(w))
            free[w] = [x]
            xe, te, se = (v.rearrange("p (c two) -> p c two", two=2) for v in (qk[w][:], rtmp[w][:], sinb[:]))
            tt("vector", "rope_sin", te[:, :, 0], xe[:, :, 1], se[:, :, 0], ALU.mult, x, rope_done.get(w))
            m = tt("vector", "rope_sin", te[:, :, 1], xe[:, :, 0], se[:, :, 1], ALU.mult, x, rope_done.get(w))
            rope_done[w] = tt("gpsimd", "rope_cos", qk[w][:], qk[w][:], cosb[:], ALU.mult, m)

        def d_rope(w):
            rope_done[w] = tt("vector", "rope_done", qk[w][:], qk[w][:], rtmp[w][:], ALU.add, rope_done[w])

        def d_v(t):
            r = t % 2
            v = tt("vector", "v2_done", vn[r][:], bank[2], absb[2][:], ALU.add, qkv_psum[t, 2], t_d, vbd_ready.get(t - 2))
            free[2] = [v]
            for b2 in range(2):
                for j2 in range(2):
                    vbd_ready[t] = dma(f"vbd_loaded{r}", Vbd[r][64 * j2:64 * j2 + 64, b2, :, 64 * j2:64 * j2 + 64],
                                       vn[r][64 * b2:64 * b2 + 64, :].rearrange("p (j z) -> p j z", j=4)[:, :, 64 * j2:64 * j2 + 64],
                                       v, t_z2, o2_psum.get((t - 2, 1)))

        def d_turn(t):
            r = t % 2
            for w in range(2):
                tr = transposes("qkT_psum", bank[3 + w], [qk[w][:, g * P:(g + 1) * P] for g in range(4)], rope_done[w], *free[3 + w])
                qk_read[w] = tr
                if w == 0:
                    src = bank[3].rearrange("p (g b q) -> p b g q", g=4, b=2)
                    for h in range(4):
                        rs = slice(32 * h, 32 * h + 32)
                        dst = qbd2[r][rs, :, h // 2:8:2, 64 * (h % 2):64 * (h % 2) + 64]
                        c = copy_act("qbd2_done", dst, src[rs], tr, t_z2, s2_psum.get((t - 2, 1)))
                    qb_ready[t] = c
                else:
                    c = kt2_ready[t] = copy_act("kT2_done", kT2[r][:], bank[4].rearrange("p (g q) -> p g q", g=4), tr, s2_psum.get((t - 2, 1)))
                free[3 + w] = [c]

        def d_turn_p(t, b2):
            flat = P2[b2][:].rearrange("p j k -> p (j k)")
            p2_read[b2] = transposes("p2T_psum", bank[3 + b2], [flat[:, g * P:(g + 1) * P] for g in range(4)], p2_ready[t, b2], *free[3 + b2])
            pt2_ready[t, b2] = copy_act("p2T_done", PT2[b2][:], bank[3 + b2], p2_read[b2], o2_psum.get((t - 1, b2)))
            free[3 + b2] = [pt2_ready[t, b2]]

        def d_weigh(t):
            for b2 in range(2):
                def emit(e, b2=b2):
                    for g in range(4):
                        mm = e.matmul(bank[1 + b2][:, g * P:(g + 1) * P], Vbd[t % 2][:, b2, g, :], PT2[b2][:, g * P:(g + 1) * P], start=True, stop=True)
                    return mm
                o2_psum[t, b2] = run("tensor", "o2_psum", [pt2_ready[t, b2], vbd_ready[t], *free[1 + b2]], emit)
            both = psum[:, 1:3, :].rearrange("p b (g h q) -> p b g h q", g=4, h=2)
            for h in range(4):
                rs = slice(32 * h, 32 * h + 32)
                c = copy_act("o2_copy", o2f[rs, :, :].rearrange("p g (b q) -> p b g q", b=2), both[rs, :, :, h % 2, :], o2_psum[t, 1], o2f_read.get(t - 1))
            free[1], free[2] = [c], [c]
            hi = copy_act("o2_hi", o2[0][:], o2f[:], c, o2_read.get(t - 1))
            o2_ready[t] = o2f_read[t] = tt("vector", "o2_lo", o2[1][:], o2f[:], o2[0][:], ALU.subtract, hi)

        def d_out(t):
            ps = products("d_psum", bank[0], split_pairs([pair(o2, slice(None), g) for g in range(4)],
                                                        [pair(Wa[3], slice(None), g) for g in range(4)]),
                          o2_ready[t], *t_wa[6:8], *free[0])
            o2_read[t] = ps
            x2_done[t] = tt("vector", "x2_done", x1[:, t, :], bank[0], x1[:, t, :], ALU.add, ps, x1_bias[t])
            free[0] = [x2_done[t]]
            x2_stat[t] = ln_stats(x1[:, t, :], t % 2, x2_done[t])

        x2_stat, x2n_stored, x2T_psum, x2T_ready, lg_psum, wgt_done, acc_mm, out_seeded = {}, {}, {}, {}, {}, {}, {}, [None]

        def d_normal(t):
            n = ln_apply("e_norm", x1[:, t, :], nx2[:], t % 2, x2_stat[t], x2T_psum.get(t - 1), x2n_stored.get(t - 1))
            x2n_stored[t] = dma("x2n_stored", x2n_dram[t * P:(t + 1) * P, :], nx2[:], n)
            x2n_done[t] = n

        x2n_done = {}

        def d_turn_x2(t):
            tr = transposes("x2T_psum", bank[7], [nx2[:, k * P:(k + 1) * P] for k in range(KD)], x2n_done[t], *free[7])
            x2T_psum[t] = tr
            x2T_ready[t] = copy_act("x2T_done", x2c[:], bank[7].rearrange("p (k q) -> p k q", k=KD), tr, lg_psum.get(t - 1))
            free[7] = [x2T_ready[t]]

        def logits(t):
            ps = products("lg_psum", bank[7][:, 0:P], [(x2c[:, k, :], wrp[:, k, :]) for k in range(KD)], x2T_ready[t], t_e, *free[7])
            lg_psum[t] = ps

        def route(t):
            lg, top, ex, mk, sm, ng = (rt[:, i, :] for i in range(6))
            x = tt("vector", "route", lg, bank[7][:, 0:E], brb[:], ALU.add, lg_psum[t], t_e, wgt_done.get(t - 1))
            free[7] = [x]
            x = run("vector", "route", [x], lambda e: e.max(top, lg))
            x = run("vector", "route", [x], lambda e: e.tensor_scalar(ng[:, 0:1], top[:, 0:1], -1.0, None, ALU.mult))
            ex_done = run("scalar", "route_exp", [x], lambda e: e.activation(ex, lg, ACT.Exp, bias=ng[:, 0:1]))
            m = run("vector", "route", [x], lambda e: e.tensor_scalar(mk, lg, top[:, 1:2], None, ALU.is_ge))
            m = run("vector", "route", [m], lambda e: e.tensor_copy(maskb[:, t, :], mk))
            x = tt("vector", "route", ex, ex, mk, ALU.mult, ex_done, m)
            x = run("vector", "route", [x], lambda e: e.tensor_reduce(sm[:, 0:1], ex, AX, ALU.add))
            x = run("vector", "route", [x], lambda e: e.reciprocal(sm[:, 1:2], sm[:, 0:1]))
            wgt_done[t] = run("vector", "route", [x], lambda e: e.tensor_scalar(wgt[:, t, :], ex, sm[:, 1:2], None, ALU.mult))

        def route_data(t):
            if t + 1 < NT:
                seen[t + 1] = (tt("vector", "seen", maskc[:, t + 1, :], maskc[:, t, :], maskb[:, t, :], ALU.add, wgt_done[t], seen[t]))
            x = wgt_done[t]
            rest = wgt
            for k in range(3):
                part = rowdata[:, t, :, 2 + k]
                x = run("vector", "rowdata", [x, rowdata0], lambda e, rest=rest, part=part: e.tensor_copy(part, rest[:, t, :]))
                if k < 2:
                    x = tt("vector", "rowdata", wrest[:, t, :], rest[:, t, :], part, ALU.subtract, x)
                    rest = wrest
            rowdata_done[t] = x

        rowdata_done = {}
        rowdata0 = run("gpsimd", "rowdata0", [t_e], lambda e: e.tensor_copy(rowdata[:], rowcol[:].unsqueeze(2).to_broadcast([P, NT, E, 6])))
        seen = {0: run("gpsimd", "rowdata0", [], lambda e: e.memset(maskc[:, 0, :], 0.0))}

        def seed_turn(t):
            tr = run("tensor", "wT_psum", [wgt_done[t], *free[7]], lambda e: e.transpose(bank[7][0:E, 0:P], wgt[:, t, :], ident[:]))
            wT_ready[t] = copy_act("wT_done", wT[:], bank[7][0:E, 0:P], tr, acc_mm.get(t - 1))

        wT_ready = {}

        def seed(t):
            ps = products("seed_psum", bank[7], [(wT[:], b2s[:])], wT_ready[t], t_e)
            acc_mm[t] = ps
            s = tt("vector", "acc_done", acc[:, t, :], bank[7], acc[:, t, :], ALU.add, ps, wgt_done[t])
            free[7] = [s]
            out_seeded[0] = dma("out_seeded", out[t * P:(t + 1) * P, :], acc[:, t, :], s)
            if t < NC:
                out_seeded[0] = dma("out_seeded", out[T + t * P:T + (t + 1) * P, :], acc[:, t, :], s)

        w12 = a["W12"]
        w_slot, slot_read = {}, {}

        def slot_left(i):
            last = NT - 1
            if i < 6:
                return [qkv_psum[last, i // 2]]
            if i < 8:
                return [s2_psum[last, 1]]
            if i == 8:
                return [x1_bias[last], rope_done[0], rope_done[1], vbd_ready[last]]
            if i == 9:
                return [rope_done[1], vbd_ready[last], s2_psum[last, 1]]
            if i < 12:
                return [p2_read[0], p2_read[1], o2_psum[last, 1], qkv_psum[last, 2]]
            if i < 14:
                return [o2_read[last]]
            return [lg_psum[last], x2T_psum[last], x2n_stored[last], rope_done[0], rope_done[1], qk_read[0], qk_read[1]]

        def load_w(e, i):
            w_slot[e, i] = load_split(w12[e, i], Wh[i][0][:], Wh[i][1][:], "vector" if i % 3 == 2 else "gpsimd",
                                      *(slot_left(i) if e == 0 else [slot_read[e - 1, i]]))

        def load_ahead(n):
            if i >= NT:
                for _ in range(n):
                    load_w(0, len(w_slot))

        for i in range(NT + 3):
            on = lambda k: 0 <= i - k < NT
            t, ts = (i if on(0) else None), (i - 1 if on(1) else None)
            for w in range(3):
                if on(0) or (on(1) and w < 2):
                    d_products(w, t, ts if w < 2 else None)
                if on(3) and w == 0:
                    d_turn_x2(i - 3)
                if on(3) and w == 1:
                    logits(i - 3)
            if on(0):
                d_bias(t, 0)
            if on(1):
                d_softmax_a(i - 1, 0)
            if on(0):
                d_rope(0)
            load_ahead(1)
            if on(1):
                d_softmax_b(i - 1, 0)
            if on(0):
                d_bias(t, 1)
            if on(1):
                d_softmax_a(i - 1, 1)
            if on(3):
                route(i - 3)
            if on(0):
                d_rope(1)
            load_ahead(1)
            if on(1):
                d_softmax_b(i - 1, 1)
            if on(0):
                d_v(t)
                x1_bias[t] = tt("gpsimd", "x1_bias", x1[:, t, :], x1[:, t, :], absb[3][:], ALU.add, *c_done, t_d)
            if on(2):
                d_out(i - 2)
            if on(1):
                d_turn_p(i - 1, 0)
                d_turn_p(i - 1, 1)
            if on(3):
                seed_turn(i - 3)
            if on(0):
                d_turn(t)
            load_ahead(1)
            if on(1):
                d_weigh(i - 1)
            if on(3):
                seed(i - 3)
                route_data(i - 3)
            if on(2):
                d_normal(i - 2)
            load_ahead(1)
        d_done = [out_seeded[0], o2_read[NT - 1], x2T_psum[NT - 1], o2_psum[NT - 1, 1], wgt_done[NT - 1], o2_ready[NT - 1],
                  rowdata_done[NT - 1], x2T_ready[NT - 1], acc_mm[NT - 1], *free[7], lg_psum[NT - 1], x2n_stored[NT - 1], t_z2]

        def emit_rank(e):
            for t in range(NT):
                e.matmul(bank[7][:, t * E:(t + 1) * E], before[:], maskb[:, t, :], start=True, stop=False)
                e.matmul(bank[7][:, t * E:(t + 1) * E], ones[:], maskc[:, t, :], start=False, stop=True)
            for n, m in enumerate((maskb, maskc)):
                mm = e.matmul(bank[7][:, NT * E:(NT + 1) * E], ones[:], m[:, NT - 1, :], start=n == 0, stop=n == 1)
            return mm
        rk = run("tensor", "rank_psum", [wgt_done[NT - 1], seen[NT - 1], t_e, *free[7]], emit_rank)
        flat_mask = maskb[:].rearrange("p t e -> p (t e)")
        x = run("vector", "rank_done", [rk], lambda e: e.scalar_tensor_tensor(rank0[:], bank[7][:, 0:NT * E], 1.0, flat_mask, ALU.add, ALU.mult))
        t_count = run("vector", "rank_done", [rk], lambda e: e.tensor_copy(count[:], bank[7][:, NT * E:(NT + 1) * E]))
        for k in range(NW):
            t_rank = run("vector", "rank_done", [x], lambda e, k=k: e.tensor_scalar(rank[:, k, :], rank0[:], -1.0 - k * TW, None, ALU.add))
        t_rowdata = rowdata_done[NT - 1]

        h_free = {i: [*d_done, t_rank, t_count] for i in range(3)}
        y_free = {c: list(d_done) for c in range(NC)}
        found_free, xt_free = [list(d_done)], {c: list(d_done) for c in range(NC)}
        xgT_read, xgT_ready, idx_ready, gathered, xg_read, ys_stored, scattered = {}, {}, {}, {}, {}, {}, [None]
        onehot_ready, onehot_read = [None], [None]
        state = {"h": 0, "g_last": {}, "hs_last": {}, "hs_read": {}}

        def buffer_of(e, k):
            return e % 2 if k == 0 else 2

        def find_a(e_, k):
            for t in range(NT):
                col = t * E + e_
                x = run("vector", "onehot", [t_rank, onehot_read[0], *(d_done if onehot_read[0] is None else [])],
                        lambda e, t=t, col=col: e.tensor_scalar(onehot[:, t, :], iota[:], rank[:, k, col:col + 1], None, ALU.is_equal))
            onehot_ready[0] = x

        def find_b(e_, k):
            r = buffer_of(e_, k)

            def emit(e):
                for c in range(NC):
                    for t in range(NT):
                        mm = e.matmul(bank[5][:, 8 * c:8 * c + 6], onehot[:, t, c * P:(c + 1) * P], rowdata[:, t, e_, :],
                                      start=t == 0, stop=t == NT - 1)
                return mm
            ps = run("tensor", "found_psum", [onehot_ready[0], t_rowdata, *found_free[0]], emit)
            onehot_read[0] = ps
            x = run("vector", "found", [ps], lambda e: e.tensor_copy(found[:], bank[5][:, 0:8 * NC].rearrange("p (c z) -> p c z", c=NC)[:, :, 0:6]))
            found_free[0] = [x]
            f = lambda z: found[:, :, z]
            old = [gathered.get(r), scattered[0]]
            row = run("vector", "found", [x], lambda e: e.scalar_tensor_tensor(rowid[:, 0, :], f(0), float(P), f(1), ALU.mult, ALU.add))
            w = tt("vector", "found", rowid[:, 1, :], f(2), f(3), ALU.add, x)
            u = tt("vector", "found", rowid[:, 2, :], f(5), dump[:], ALU.mult, x)
            g = run("vector", "found", [row, *old], lambda e: e.tensor_copy(gidx[r][:], rowid[:, 0, :]))
            v = tt("vector", "found", rowid[:, 3, :], rowid[:, 0, :], dump[:], ALU.add, row)
            w = tt("vector", "found", gw[r][:], rowid[:, 1, :], f(4), ALU.add, w, *ys_stored.values())
            v = tt("vector", "found", sidx[r][:], rowid[:, 3, :], rowid[:, 2, :], ALU.subtract, v, u, *old)
            idx_ready[e_, k] = v
            for c in range(NC):
                b = 2 * (k % 2) + c
                gathered[r] = run("gpsimd", f"gathered{k % 2}", [g, *x2n_stored.values(), xg_read.get(b), out_seeded[0]],
                                  lambda e, c=c, b=b: e.indirect_dma_start(xg[b][:], None, x2n_dram, bass.IndirectOffsetOnAxis(gidx[r][:, c:c + 1], 0)), step=16)
            gathered[e_, k] = gathered[r]

        def find_c(e_, k):
            r = buffer_of(e_, k)
            for c in range(NC):
                b = 2 * (k % 2) + c
                tr = transposes("xgT_psum", bank[6 + c], [xg[b][:, q * P:(q + 1) * P] for q in range(KD)], gathered[e_, k], *xt_free[c])
                xg_read[b] = tr
                src = bank[6 + c][:].rearrange("p (k q) -> p k q", k=KD)
                dst = [z[:, :, c * P:(c + 1) * P] for z in xgT[r]]
                hi = copy_act("xgT_hi", dst[0], src, tr, xgT_read.get(r), *(d_done if e_ == 0 else []))
                lo = tt("vector", "xgT_lo", dst[1], src, dst[0], ALU.subtract, hi)
                xt_free[c] = [lo]
            xgT_ready[e_, k] = lo

        def up(e_, k, i):
            r = buffer_of(e_, k)
            n = state["h"]
            state["h"] += 1
            bk = bank[n % 3]
            ps = products("h_psum", bk[:, 0:TW], split_pairs([(Wh[i][0][:, q * P:(q + 1) * P], Wh[i][1][:, q * P:(q + 1) * P]) for q in range(KD)],
                                                            [pair(xgT[r], slice(None), q) for q in range(KD)]),
                          w_slot[e_, i], xgT_ready[e_, k], *h_free[n % 3])
            xgT_read[r] = ps
            col = e_ * NI + i
            g = run("scalar", "gelu", [ps, state["g_last"].get(n % 2), t_cols, *(d_done if n < 2 else [])],
                    lambda e: e.activation(gl[n % 2][:], bk[:, 0:TW], ACT.Gelu, bias=b1c[:, col:col + 1]))
            h_free[n % 3] = [g]
            hi = run("vector", "h_hi", [g, state["hs_read"].get(n % 3), *(d_done if n < 3 else [])],
                     lambda e: e.tensor_copy(hs[n % 3][0][:], gl[n % 2][:]))
            lo = tt("vector", "h_lo", hs[n % 3][1][:], gl[n % 2][:], hs[n % 3][0][:], ALU.subtract, hi)
            state["g_last"][n % 2] = state["hs_last"][n % 3] = lo
            return n

        def down(e_, k, i, n):
            r = buffer_of(e_, k)
            hr = hs[n % 3]

            def emit(e):
                for c in range(NC):
                    for m, (x, y) in enumerate(((0, 0), (0, 1), (1, 0))):
                        mm = e.matmul(bank[3 + c][:], hr[x][:, c * P:(c + 1) * P], Wh[i][y][:, 512:1024],
                                      start=i == 0 and m == 0, stop=i == NI - 1 and m == 2)
                return mm
            ps = run("tensor", "y_psum", [state["hs_last"][n % 3], *(sum(y_free.values(), []) if i == 0 else [])], emit)
            state["hs_read"][n % 3] = ps
            slot_read[e_, i] = ps
            if i == NI - 1:
                last = scattered[0]
                for c in range(NC):
                    s = run("scalar", "y_done", [ps, idx_ready[e_, k], ys_stored.get(c), *(d_done if e_ == 0 else [])],
                            lambda e, c=c: e.activation(ys[c][:], bank[3 + c][:], ACT.Copy, scale=gw[r][:, c:c + 1]))
                    y_free[c] = [s]
                    scattered[0] = run("gpsimd", "out_added", [s, last, out_seeded[0]], lambda e, c=c: e.indirect_dma_start(
                        out, bass.IndirectOffsetOnAxis(sidx[r][:, c:c + 1], 0), ys[c][:], None, compute_op=ALU.add), step=16)
                for c in range(NC):
                    ys_stored[c] = scattered[0]

        def expert_tile(e_, k, between):
            ns = {}
            for i in range(NI + 1):
                if i < NI:
                    ns[i] = up(e_, k, i)
                if i >= 1:
                    down(e_, k, i - 1, ns[i - 1])
                    if k == 0 and e_ + 1 < E:
                        load_w(e_ + 1, i - 1)
                for fn in between.get(i, ()):
                    fn()

        ring["size"] = len(raw)
        raw_used[3:] = [out_seeded[0]] * 3
        find_a(0, 1)
        find_b(0, 1)
        find_a(0, 0)
        find_b(0, 0)
        find_c(0, 1)
        load_w(0, len(w_slot))
        find_c(0, 0)
        while len(w_slot) < NI:
            load_w(0, len(w_slot))
        skipped = nc.dram_tensor("skipped", (3, P, 8), F32).ap()
        for n, name in enumerate(("gathered0", "gathered1", "out_added")):
            pg.skip_copies[pg.stage(name, 16)] = (ident[:, 0:8], skipped[n])
        pg.close("gpsimd", [t_ident])
        for e_ in range(E):
            pg.load_value("rows", ("tensor", "vector", "scalar", "gpsimd"), count[0:1, e_:e_ + 1], T, t_count)
            pg.begin_optional(lambda v: v["rows"] > TW)
            expert_tile(e_, 1, {})
            pg.end_optional()
            pg.begin_optional(lambda v: v["rows"] > 2 * TW)
            for k in range(2, NW):
                find_a(e_, k)
                find_b(e_, k)
                find_c(e_, k)
                expert_tile(e_, k, {})
            pg.end_optional()
            if e_ + 1 < E:
                n_ = e_ + 1
                expert_tile(e_, 0, {1: [lambda: find_a(n_, 0)], 3: [lambda: find_b(n_, 0)], 6: [lambda: find_c(n_, 0)],
                                    8: [lambda: find_a(n_, 1)], 10: [lambda: find_b(n_, 1)], 13: [lambda: find_c(n_, 1)]})
            else:
                expert_tile(e_, 0, {})
        pg.close("gpsimd", [scattered[0]])

        pg.emit_all(stack.enter_context(nc.Block()))


def rope_tables():
    hd, dim, frame, grid = 32, 10, 256, 16
    pos = np.arange(128) % 64
    f = pos // frame
    rem = pos - frame * f
    cos = np.ones((128, hd), np.float32)
    sin = np.zeros((128, hd), np.float32)
    inv = (np.float32(1.0) / np.float32(10000.0) ** (np.arange(dim // 2, dtype=np.float32) / np.float32(dim / 2.0))).astype(np.float32)
    for axis, ids in enumerate((f, rem // grid, rem % grid)):
        freq = ids.astype(np.float32)[:, None] * inv
        cos[:, axis * dim:(axis + 1) * dim] = np.concatenate([np.cos(freq), np.cos(freq)], -1)
        sin[:, axis * dim:(axis + 1) * dim] = np.concatenate([np.sin(freq), np.sin(freq)], -1)
    sin[:, 0::2] *= -1
    return np.tile(cos, (1, 16)), np.tile(sin, (1, 16))


def routing_tables():

    bf16 = mybir.dt.np(BF16)
    rowcol = np.zeros((128, 8, 6), np.float32)
    rowcol[:, :, 0] = np.arange(8)
    rowcol[:, :, 1] = np.arange(128)[:, None]
    rowcol[:, :, 5] = 1
    return {
        "iota": np.broadcast_to(np.arange(256), (128, 256)).astype(bf16),
        "before": np.triu(np.ones((128, 128)), 1).astype(bf16),
        "ones": np.ones((128, 128), bf16),
        "rowcol": rowcol,
        "dump": (1024 + np.arange(2)[None, :] * 128 + np.arange(128)[:, None]).astype(np.float32),
    }


def kernel(**inputs):
    import concourse.bacc as bacc
    from concourse.bass_utils import run_bass_kernel_spmd

    g = {k: np.asarray(v) for k, v in inputs.items()}
    E, D, HID = g["L0_ffn_W1"].shape
    cols = lambda v: np.ascontiguousarray(v.reshape(-1, 128).T)
    cos, sin = rope_tables()
    w1 = g["L0_ffn_W1"].reshape(E, D // 128, 128, HID // 128, 128).transpose(0, 3, 2, 1, 4).reshape(E, HID // 128, 128, D)
    w2 = g["L0_ffn_W2"].reshape(E, HID // 128, 128, D)
    arrays = {
        "x": g["x"].reshape(-1, D),
        "ctxT": g["ctx_1024"].transpose(0, 2, 1).reshape(16, D // 128, 128, 512).transpose(0, 2, 1, 3),
        "Wq": g["L0_xattn_Wq"], "Wk": g["L0_xattn_Wk"], "Wv": g["L0_xattn_Wv"], "Wo": g["L0_xattn_Wo"],
        "bq": cols(g["L0_xattn_bq"]), "bk": cols(g["L0_xattn_bk"]), "bv": g["L0_xattn_bv"], "bo": g["L0_xattn_bo"],
        "gamma": g["L0_xattn_ln_gamma"], "beta": g["L0_xattn_ln_beta"],
        "aWq": g["L0_attn_Wq"], "aWk": g["L0_attn_Wk"], "aWv": g["L0_attn_Wv"], "aWo": g["L0_attn_Wo"],
        "abq": g["L0_attn_bq"], "abk": g["L0_attn_bk"], "abv": g["L0_attn_bv"], "abo": g["L0_attn_bo"],
        "W12": np.concatenate([w1, w2], -1), "b1": cols(g["L0_ffn_b1"]), "b2": g["L0_ffn_b2"],
        "Wr": g["L0_ffn_Wr"], "br": g["L0_ffn_br"],
        "cos": cos, "sin": sin, "ident": np.eye(128, dtype=np.float32),
        **routing_tables(),
    }
    arrays = {k: np.ascontiguousarray(v) for k, v in arrays.items()}
    nc = bacc.Bacc("TRN2", target_bir_lowering=False, num_devices=1)
    aps = {k: nc.dram_tensor(f"in_{k}", v.shape, mybir.dt.from_np(v.dtype), kind="ExternalInput").ap() for k, v in arrays.items()}
    rows = g["x"].shape[0] * g["x"].shape[1]
    out = nc.dram_tensor("out_x", (rows + 256, D), F32, kind="ExternalOutput").ap()
    perceiver_block(nc, aps, out)
    r = run_bass_kernel_spmd(nc, [{f"in_{k}": v for k, v in arrays.items()}], core_ids=[0])
    return r.results[0]["out_x"][:rows].reshape(g["x"].shape)
```
